# Optimizing a Trainium2 kernel written in Bass

```python
import numpy as np
import jax
import jax.numpy as jnp

def _softmax(x, axis=-1):
    return jax.nn.softmax(x, axis=axis)

def _gelu(x):
    return jax.nn.gelu(x, approximate=True)

def _silu(x):
    return jax.nn.silu(x)

def _sigmoid(x):
    return jax.nn.sigmoid(x)

def _layernorm(x, axis=-1, eps=1e-05):
    m = jnp.mean(x, axis=axis, keepdims=True)
    v = jnp.var(x, axis=axis, keepdims=True)
    return (x - m) / jnp.sqrt(v + eps)

def _scatter_add(tgt, idx, src, axis=0):
    return tgt.at[idx].add(src)

def _segment_sum(src, seg, n):
    return jax.ops.segment_sum(src, seg, n)
kernel_name = 'mk_seq_postln_d1_jaxref_r8_d8bcbc'

def setup_inputs(seed: int=0):
    np.random.seed(seed)
    _w = jnp.asarray

    def _L0_attn_setup():
        import jax, jax.numpy as jnp
        import numpy as np
        NUM_HEADS = 16
        key = jax.random.key(seed)
        ks = jax.random.split(key, 5)
        B, S, D = (2, 256, 128)
        q = jax.random.normal(ks[0], (B, S, D), dtype=jnp.float32)
        k = jax.random.normal(ks[1], (B, S, D), dtype=jnp.float32)
        v = jax.random.normal(ks[2], (B, S, D), dtype=jnp.float32)
        in_w = jax.random.normal(ks[3], (3 * D, D), dtype=jnp.float32) * 0.02
        qkv_bias = jnp.zeros((3 * D,), dtype=jnp.float32)
        out_w = jax.random.normal(ks[4], (D, D), dtype=jnp.float32) * 0.02
        out_b = jnp.zeros((D,), dtype=jnp.float32)
        return {'q': q, 'k': k, 'v': v, 'in_w': in_w, 'qkv_bias': qkv_bias, 'out_w': out_w, 'out_b': out_b}
    _L0_attn_in = _L0_attn_setup()

    def _L0_ffn_setup():
        import jax, jax.numpy as jnp
        import numpy as np
        DIM = 128
        HIDDEN = 384
        SCALE = 1.0 / 127.0

        def _dequant(w_int, dtype):
            return w_int.astype(dtype) * jnp.asarray(SCALE, dtype)
        key = jax.random.key(seed)
        k_x, k_g, k_u, k_d = jax.random.split(key, 4)
        x = jax.random.normal(k_x, (4, 256, DIM), dtype=jnp.float32)
        w_gate = jax.random.randint(k_g, (HIDDEN, DIM), -127, 128, dtype=jnp.int32)
        w_up = jax.random.randint(k_u, (HIDDEN, DIM), -127, 128, dtype=jnp.int32)
        w_down = jax.random.randint(k_d, (DIM, HIDDEN), -127, 128, dtype=jnp.int32)
        return {'x': x, 'w_gate': w_gate, 'w_up': w_up, 'w_down': w_down}
    _L0_ffn_in = _L0_ffn_setup()
    _d = {'L0_attn_q': _L0_attn_in['q'], 'L0_attn_k': _L0_attn_in['k'], 'L0_attn_v': _L0_attn_in['v'], 'L0_attn_in_w': _L0_attn_in['in_w'], 'L0_attn_qkv_bias': _L0_attn_in['qkv_bias'], 'L0_attn_out_w': _L0_attn_in['out_w'], 'L0_attn_out_b': _L0_attn_in['out_b'], 'L0_ffn_w_gate': _L0_ffn_in['w_gate'], 'L0_ffn_w_up': _L0_ffn_in['w_up'], 'L0_ffn_w_down': _L0_ffn_in['w_down']}
    _x0 = _d['L0_attn_q']
    _d['L0_attn_q'] = jax.random.normal(jax.random.fold_in(jax.random.key(seed), 1), (8, 512, 128), dtype=_x0.dtype)
    del _x0
    return _d

def reference(L0_attn_q, L0_attn_k, L0_attn_v, L0_attn_in_w, L0_attn_qkv_bias, L0_attn_out_w, L0_attn_out_b, L0_ffn_w_gate, L0_ffn_w_up, L0_ffn_w_down):

    def _L0_attn_ref(q, k, v, in_w, qkv_bias, out_w, out_b):
        import jax, jax.numpy as jnp
        import numpy as np
        NUM_HEADS = 16
        B, S, D = q.shape
        H = NUM_HEADS
        hd = D // H
        scaling = float(hd) ** 0.5
        qkv = q @ in_w.T + qkv_bias
        qp, kp, vp = jnp.split(qkv, 3, axis=-1)

        def to_heads(t):
            return t.reshape(B, S, H, hd).transpose(0, 2, 1, 3)
        qh, kh, vh = (to_heads(qp), to_heads(kp), to_heads(vp))
        scores = jnp.einsum('bhsd,bhtd->bhst', qh, kh) / scaling
        weights = jax.nn.softmax(scores, axis=-1)
        out = jnp.einsum('bhst,bhtd->bhsd', weights, vh)
        out = out.transpose(0, 2, 1, 3).reshape(B, S, D)
        net = out @ out_w.T + out_b
        return net

    def _L0_ffn_ref(x, w_gate, w_up, w_down):
        import jax, jax.numpy as jnp
        import numpy as np
        DIM = 128
        HIDDEN = 384
        SCALE = 1.0 / 127.0

        def _dequant(w_int, dtype):
            return w_int.astype(dtype) * jnp.asarray(SCALE, dtype)
        wg = _dequant(w_gate, x.dtype)
        wu = _dequant(w_up, x.dtype)
        wd = _dequant(w_down, x.dtype)
        gate = jnp.einsum('bsd,hd->bsh', x, wg)
        up = jnp.einsum('bsd,hd->bsh', x, wu)
        h = jax.nn.silu(gate) * up
        return jnp.einsum('bsh,dh->bsd', h, wd)
    x = L0_attn_q
    x = _layernorm(x + _L0_attn_ref(x, L0_attn_k, L0_attn_v, L0_attn_in_w, L0_attn_qkv_bias, L0_attn_out_w, L0_attn_out_b), axis=-1)
    x = _layernorm(x + _L0_ffn_ref(x, L0_ffn_w_gate, L0_ffn_w_up, L0_ffn_w_down), axis=-1)
    return x

_drawn_inputs = setup_inputs


def setup_inputs(seed=0):
    import zlib

    import numpy as np

    out = dict(_drawn_inputs(seed))
    spreads = {'L0_attn_qkv_bias': (0.0, 0.1), 'L0_attn_out_b': (0.0, 0.1)}
    factors = {'L0_attn_in_w': 8.0}
    for name, (base, spread) in spreads.items():
        noise = np.random.default_rng([zlib.crc32(name.encode()), seed]).standard_normal(out[name].shape)
        drawn = base * np.exp(spread * noise) if base else spread * noise
        out[name] = jnp.asarray(drawn.astype(out[name].dtype))
    for name, factor in factors.items():
        out[name] = (out[name] * factor).astype(out[name].dtype)
    return out
```

```python
from contextlib import ExitStack

import concourse.bass as bass
from concourse import mybir

ALU = mybir.AluOpType
ACT = mybir.ActivationFunctionType
AX = mybir.AxisListType
F32 = mybir.dt.float32
BF16 = mybir.dt.bfloat16
I32 = mybir.dt.int32

P = 128
H = 16
HD = 8
G = 4
J = H // G
NT = 4
EPS = 1e-5
WEIGHT_SCALE = 1.0 / 127.0
PRODUCTS = 6
ROWS = HD * PRODUCTS
SHIFT_ROW = 96
SCORE_ROWS = 96
OROWS = 32


def transformer_layer(nc, x, in_w, qkv_bias, out_w, out_b, w_gate, w_up, w_down, out):
    B, S, D = x.shape
    HID = w_gate.shape[0]
    C = HID // P
    assert D == P and S == NT * P and HID == C * P and D == H * HD
    SCALING = float(HD) ** 0.5

    q_scratch = nc.dram_tensor("q_scratch", (B, P, PRODUCTS, S), BF16, kind="Internal").ap()
    k_scratch = nc.dram_tensor("k_scratch", (B, P, PRODUCTS, S), BF16, kind="Internal").ap()
    o_scratch = nc.dram_tensor("o_scratch", (B, H, OROWS, S), F32, kind="Internal").ap()
    r_scratch = nc.dram_tensor("r_scratch", (B, H, S), F32, kind="Internal").ap()

    x_rows = x.rearrange("b (t p) d -> b p t d", p=P)
    out_rows = out.rearrange("b (t p) d -> b p t d", p=P)
    q_stacks = q_scratch.rearrange("b (g j d) c s -> b g (d c) j s", g=G, j=J)
    k_stacks = k_scratch.rearrange("b (g j d) c s -> b g (d c) j s", g=G, j=J)

    with ExitStack() as ctx:
        def sb(name, shape, dt=F32):
            return ctx.enter_context(nc.sbuf_tensor(name, shape, dt))

        def psum(name, shape):
            return ctx.enter_context(nc.psum_tensor(name, shape, F32))

        def sem(name):
            return ctx.enter_context(nc.semaphore(name))

        ident = sb("ident", [P, P])
        in_w_sb = sb("in_w_sb", [P, 3, P])
        out_w_sb = sb("out_w_sb", [P, P])
        w_int = sb("w_int", [P, 3, C, P], I32)
        w_deq = sb("w_deq", [P, 3, C, P])
        wT = sb("wT", [P, 4, P])
        gateT = sb("gateT", [P, C * P])
        upT = sb("upT", [P, C * P])
        downT = sb("downT", [P, C, P])
        bias_col = sb("bias_col", [P, 3])
        bias_q = sb("bias_q", [P, 1])
        v_bias = sb("v_bias", [P, P])
        o_bias = sb("o_bias", [P, P])
        minus_half = sb("minus_half", [P, NT])
        eps = sb("eps", [P, NT])
        one = sb("one", [P, 1])
        x_in = sb("x_in", [P, NT, P])
        xT = sb("xT", [P, S])
        q_full = sb("q_full", [P, S])
        k_full = sb("k_full", [P, S])
        q_rest = sb("q_rest", [P, S])
        k_rest = sb("k_rest", [P, S])
        q_parts = sb("q_parts", [P, 3, S], BF16)
        k_parts = sb("k_parts", [P, 3, S], BF16)
        v_rows = sb("v_rows", [P, NT, P])
        q_stack = sb("q_stack", [P, G, J, S], BF16)
        k_stack = sb("k_stack", [P, G, J, S], BF16)
        v_ones = sb("v_ones", [P, G, NT, J, OROWS])
        neg_max = sb("neg_max", [P, 2, J * NT])
        shift_parts = sb("shift_parts", [J * NT, 2, P], BF16)
        probs = sb("probs", [P, 2, J, S])
        o_raw = sb("o_raw", [P, 2, S])
        oT = sb("oT", [P, S])
        sums = sb("sums", [P, H * S // P])
        recips = sb("recips", [P, H * S // P])
        recip_rows = sb("recip_rows", [P, S])
        oT_norm = sb("oT_norm", [P, S])
        x_again = sb("x_again", [P, NT, P])
        x_biased = sb("x_biased", [P, NT, P])
        y1 = sb("y1", [P, NT, P])
        y2 = sb("y2", [P, NT, P])
        stats = sb("stats", [P, NT, 6])
        mean_var = sb("mean_var", [P, NT, 2])
        var_eps = sb("var_eps", [P, NT])
        rstd = sb("rstd", [P, NT])
        x1 = sb("x1", [P, NT, P])
        x1T = sb("x1T", [P, S])
        tanh = sb("tanh", [P, S])
        gated = sb("gated", [P, S])
        hidden = sb("hidden", [P, C, S])
        result = sb("result", [P, NT, P])

        ps_b = psum("ps_b", [P, J, S])
        ps_a = psum("ps_a", [P, 2, S])
        ps_o = psum("ps_o", [P, S])
        ps_m = psum("ps_m", [P, S])

        w_loaded = sem("w_loaded")
        bias_loaded = sem("bias_loaded")
        x_loaded = sem("x_loaded")
        ident_zero = sem("ident_zero")
        ident_made = sem("ident_made")
        stacks_zero = sem("stacks_zero")
        const_made = sem("const_made")
        bias_q_made = sem("bias_q_made")
        w_scaled = sem("w_scaled")
        w_transposed = sem("w_transposed")
        w_ready = sem("w_ready")
        xT_made = sem("xT_made")
        xT_kept = sem("xT_kept")
        q_made = sem("q_made")
        k_made = sem("k_made")
        q_kept = sem("q_kept")
        k_kept = sem("k_kept")
        q_chain = sem("q_chain")
        k_chain = sem("k_chain")
        v_made = sem("v_made")
        v_kept = sem("v_kept")
        v_filled = sem("v_filled")
        q_stored = sem("q_stored")
        k_stored = sem("k_stored")
        stack_filled = [sem(f"stack_filled{g}") for g in range(G)]
        shift_filled = [sem(f"shift_filled{g}") for g in range(G)]
        a_scored = sem("a_scored")
        a_reduced = sem("a_reduced")
        shift_turned = sem("shift_turned")
        shift_split = sem("shift_split")
        b_scored = sem("b_scored")
        exp_done = sem("exp_done")
        pv_done = sem("pv_done")
        o_kept = sem("o_kept")
        o_stored = [sem(f"o_stored{n}") for n in range(2)]
        o_loaded = sem("o_loaded")
        recip_done = sem("recip_done")
        recip_stored = sem("recip_stored")
        recip_loaded = sem("recip_loaded")
        o_normed = sem("o_normed")
        x_reloaded = sem("x_reloaded")
        x_bias_added = sem("x_bias_added")
        out_made = sem("out_made")
        y1_made = sem("y1_made")
        y1_stats = sem("y1_stats")
        y1_mv = sem("y1_mv")
        var1_ready = sem("var1_ready")
        rstd1_ready = sem("rstd1_ready")
        x1_made = sem("x1_made")
        x1T_made = sem("x1T_made")
        x1T_kept = sem("x1T_kept")
        gate_made = sem("gate_made")
        tanh_done = sem("tanh_done")
        gated_done = sem("gated_done")
        up_made = sem("up_made")
        hidden_done = sem("hidden_done")
        down_made = sem("down_made")
        y2_made = sem("y2_made")
        y2_stats = sem("y2_stats")
        y2_mv = sem("y2_mv")
        var2_ready = sem("var2_ready")
        rstd2_ready = sem("rstd2_ready")
        result_made = sem("result_made")
        result_stored = sem("result_stored")

        LAST = B - 1

        def whole(i):
            known = isinstance(i, int)
            post = not known or i >= 1
            v_ahead = not known or i + 1 <= LAST
            proj = not known or i + 2 <= LAST
            return post, v_ahead, proj

        def exists(i, unit_ahead):
            return not isinstance(i, int) or G * i + unit_ahead < G * B

        def rounds(eng, batch_round):
            batch_round(0)
            batch_round(1)
            with eng.Fori(2, B - 2) as i:
                batch_round(i)
            batch_round(B - 2)
            batch_round(B - 1)

        block = ctx.enter_context(nc.Block())

        @block.sync
        def _(sp):
            sp.dma_start(in_w_sb[:, :, :], in_w.rearrange("(c p) d -> p c d", p=P)).then_inc(w_loaded, 16)
            sp.dma_start(out_w_sb[:, :], out_w).then_inc(w_loaded, 16)
            sp.dma_start(w_int[:, 0, :, :], w_gate.rearrange("(c p) d -> p c d", p=P)).then_inc(w_loaded, 16)
            sp.dma_start(w_int[:, 1, :, :], w_up.rearrange("(c p) d -> p c d", p=P)).then_inc(w_loaded, 16)
            sp.dma_start(w_int[:, 2, :, :], w_down.rearrange("p (c n) -> p c n", c=C)).then_inc(w_loaded, 16)
            with nc.allow_non_contiguous_dma(reason="a bias per partition, 384 numbers once"):
                sp.dma_start(bias_col[:, :], qkv_bias.rearrange("(c p) -> p c", p=P)).then_inc(bias_loaded, 16)
            bias_2d = qkv_bias.rearrange("(a n) -> a n", a=1)
            sp.dma_start(v_bias[:, :], bias_2d[:, 2 * P:3 * P].to_broadcast([P, P])).then_inc(bias_loaded, 16)
            sp.dma_start(o_bias[:, :], out_b.rearrange("(a n) -> a n", a=1).to_broadcast([P, P])
                         ).then_inc(bias_loaded, 16)

            def load_x(n):
                sp.wait_ge(xT_made, n)
                sp.dma_start(x_in[:, :, :], x_rows[n]).then_inc(x_loaded, 16)

            def store_q(n):
                sp.wait_ge(q_chain, 3 * n + 3)
                sp.dma_start(q_scratch[n, :, 0:3, :], q_parts[:, 0:3, :]).then_inc(q_stored, 16)
                sp.dma_start(q_scratch[n, :, 3:5, :], q_parts[:, 0:2, :]).then_inc(q_stored, 16)
                sp.dma_start(q_scratch[n, :, 5:6, :], q_parts[:, 0:1, :]).then_inc(q_stored, 16)

            def store_k(n):
                sp.wait_ge(k_chain, 3 * n + 3)
                sp.dma_start(k_scratch[n, :, 0:3, :], k_parts[:, 0:1, :].to_broadcast([P, 3, S])
                             ).then_inc(k_stored, 16)
                sp.dma_start(k_scratch[n, :, 3:5, :], k_parts[:, 1:2, :].to_broadcast([P, 2, S])
                             ).then_inc(k_stored, 16)
                sp.dma_start(k_scratch[n, :, 5:6, :], k_parts[:, 2:3, :]).then_inc(k_stored, 16)

            def fill_stacks(i, ahead):
                n, g = i + ahead // G, ahead % G
                if g == 0 or isinstance(i, int):
                    sp.wait_ge(q_stored, 48 * n + 48)
                    sp.wait_ge(k_stored, 48 * n + 48)
                sp.dma_start(q_stack[0:ROWS, g, :, :], q_stacks[n, g]).then_inc(stack_filled[g], 16)
                sp.dma_start(k_stack[0:ROWS, g, :, :], k_stacks[n, g]).then_inc(stack_filled[g], 16)

            def fill_shift(i, ahead):
                g = ahead % G
                sp.wait_ge(shift_split, 2 * (G * i + ahead) + 2)
                for c in range(2):
                    row = q_stack[SHIFT_ROW + c:SHIFT_ROW + c + 1, g, :, :].rearrange("o j s -> o (j s)")
                    sp.dma_start(row, shift_parts[:, c, :]).then_inc(shift_filled[g], 16)

            def store_o(i, behind):
                g = G - behind
                sp.wait_ge(o_kept, G * i + g + 1)
                sp.dma_start(o_scratch[i, J * g:J * g + J].rearrange("j r s -> (j r) s"), o_raw[:, g % 2, :]
                             ).then_inc(o_stored[g % 2], 16)

            def normalizer(n):
                sp.wait_ge(o_stored[0], 32 * n + 32)
                sp.wait_ge(o_stored[1], 32 * n + 32)
                sp.dma_start(sums[:, :], o_scratch[n, :, HD, :].rearrange("h (c w) -> h c w", c=P // H)
                             ).then_inc(o_loaded, 16)
                sp.dma_start(oT[:, :], o_scratch[n, :, 0:HD, :]).then_inc(o_loaded, 16)
                sp.wait_ge(recip_done, n + 1)
                sp.dma_start(r_scratch[n].rearrange("h (c w) -> (h c) w", c=P // H), recips[:, :]
                             ).then_inc(recip_stored, 16)
                sp.wait_ge(recip_stored, 16 * n + 16)
                sp.dma_start(recip_rows[:, :],
                             r_scratch[n].rearrange("h (o s) -> h o s", o=1).to_broadcast([H, HD, S])
                             ).then_inc(recip_loaded, 16)

            def reload_x(n):
                if not isinstance(n, int) or n >= 1:
                    sp.wait_ge(x_bias_added, n)
                sp.dma_start(x_again[:, :, :], x_rows[n]).then_inc(x_reloaded, 16)

            def store_result(n):
                sp.wait_ge(result_made, n + 1)
                sp.dma_start(out_rows[n], result[:, :, :]).then_inc(result_stored, 16)

            sp.dma_start(x_in[:, :, :], x_rows[0]).then_inc(x_loaded, 16)
            load_x(1)
            store_q(0)
            store_k(0)
            sp.wait_ge(stacks_zero, 3)
            for ahead in range(2):
                fill_stacks(0, ahead)
            fill_stacks(0, 2)
            fill_shift(0, 0)
            store_q(1)
            store_k(1)

            def batch_round(i):
                post, v_ahead, proj = whole(i)
                for g in range(G):
                    if exists(i, g + 3):
                        if not (isinstance(i, int) and i == 0 and g == 0):
                            sp.wait_ge(b_scored, 8 * (G * i + g))
                        fill_stacks(i, g + 3)
                    if g == 0 and proj:
                        load_x(i + 2)
                    if exists(i, g + 1):
                        fill_shift(i, g + 1)
                    if g > 0:
                        store_o(i, G - g + 1)
                    elif post:
                        store_o(i - 1, 1)
                    if g == 0 and post:
                        reload_x(i - 1)
                        normalizer(i - 1)
                    if g == 2 and proj:
                        store_q(i + 2)
                    if g == 3 and proj:
                        store_k(i + 2)
                if post:
                    store_result(i - 1)

            rounds(sp, batch_round)
            store_o(LAST, 1)
            reload_x(LAST)
            normalizer(LAST)
            store_result(LAST)
            sp.wait_ge(result_stored, 16 * B)

        @block.tensor
        def _(pe):
            pe.wait_ge(ident_made, 1)
            pe.wait_ge(w_loaded, 80)
            for c in range(3):
                pe.transpose(ps_b[:, 0, c * P:(c + 1) * P], in_w_sb[:, c, :], ident[:, :])
            pe.transpose(ps_b[:, 0, 3 * P:4 * P], out_w_sb[:, :], ident[:, :]).then_inc(w_transposed, 1)
            for w in range(3):
                pe.wait_ge(w_scaled, w + 1)
                for c in range(C):
                    last = pe.transpose(ps_b[:, 1 + w, c * P:(c + 1) * P], w_deq[:, w, c, :], ident[:, :])
                last.then_inc(w_transposed, 1)

            def turn_x(n):
                pe.wait_ge(x_loaded, 16 * n + 16)
                for t in range(NT):
                    last = pe.transpose(ps_m[:, t * P:(t + 1) * P], x_in[:, t, :], ident[:, :])
                last.then_inc(xT_made, 1)

            def project_q(n):
                pe.wait_ge(xT_kept, n + 1)
                pe.matmul(ps_m[:, :], wT[:, 0, :], xT[:, :], start=True, stop=True).then_inc(q_made, 1)

            def project_k(n):
                pe.wait_ge(q_kept, 2 * n + 2)
                pe.matmul(ps_m[:, :], wT[:, 1, :], xT[:, :], start=True, stop=True).then_inc(k_made, 1)

            def project_v():
                for t in range(NT):
                    last = pe.matmul(ps_m[:, t * P:(t + 1) * P], xT[:, t * P:(t + 1) * P], wT[:, 2, :],
                                     start=True, stop=True)
                last.then_inc(v_made, 1)

            def score_a(i, ahead, t, j):
                g = ahead % G
                a = 16 * (G * i + ahead) + 4 * t + j
                if not isinstance(a, int) or a >= 2:
                    pe.wait_ge(a_reduced, a - 1)
                pe.matmul(ps_a[:, j % 2, :], q_stack[0:SCORE_ROWS, g, j, t * P:(t + 1) * P],
                          k_stack[0:SCORE_ROWS, g, j, :], start=True, stop=True).then_inc(a_scored, 1)

            def wait_stack(i, ahead):
                pe.wait_ge(stack_filled[ahead % G], 32 * (i + ahead // G) + 32)

            def score_b(g, t, r):
                for j in (2 * r, 2 * r + 1):
                    last = pe.matmul(ps_b[:, j, :], k_stack[:, g, j, t * P:(t + 1) * P], q_stack[:, g, j, :],
                                     start=True, stop=True)
                last.then_inc(b_scored, 1)

            def weigh_values(i, slot):
                g, t = slot // NT, slot % NT
                pe.wait_ge(exp_done, 2 * (16 * i + slot) + 2)
                if t == 0:
                    pe.wait_ge(v_filled, G * i + g + 1)
                    if not isinstance(i, int) or G * i + g >= 1:
                        pe.wait_ge(o_kept, G * i + g)
                for j in range(J):
                    last = pe.matmul(ps_o[OROWS * j:OROWS * j + OROWS, :], v_ones[:, g, t, j, :],
                                     probs[:, t % 2, j, :], start=(t == 0), stop=(t == NT - 1))
                last.then_inc(pv_done, 1)

            def turn_shift(i, ahead):
                pe.wait_ge(a_reduced, 16 * (G * i + ahead) + 16)
                pe.transpose(ps_m[0:J * NT, 0:P], neg_max[:, ahead % 2, :], ident[:, :]).then_inc(shift_turned, 1)

            def project_out(n):
                pe.wait_ge(o_normed, n + 1)
                for t in range(NT):
                    last = pe.matmul(ps_m[:, t * P:(t + 1) * P], oT_norm[:, t * P:(t + 1) * P], wT[:, 3, :],
                                     start=True, stop=True)
                last.then_inc(out_made, 1)

            def turn_x1(n):
                pe.wait_ge(x1_made, n + 1)
                for t in range(NT):
                    last = pe.transpose(ps_m[:, t * P:(t + 1) * P], x1[:, t, :], ident[:, :])
                last.then_inc(x1T_made, 1)

            def gate(n, c):
                if c == 0:
                    pe.wait_ge(x1T_kept, n + 1)
                else:
                    pe.wait_ge(hidden_done, C * n + c)
                pe.matmul(ps_m[:, :], gateT[:, c * P:(c + 1) * P], x1T[:, :], start=True, stop=True
                          ).then_inc(gate_made, 1)

            def up(n, c):
                pe.wait_ge(gated_done, C * n + c + 1)
                pe.matmul(ps_m[:, :], upT[:, c * P:(c + 1) * P], x1T[:, :], start=True, stop=True
                          ).then_inc(up_made, 1)

            def down(n):
                pe.wait_ge(hidden_done, C * n + C)
                for t in range(NT):
                    for c in range(C):
                        last = pe.matmul(ps_m[:, t * P:(t + 1) * P], hidden[:, c, t * P:(t + 1) * P],
                                         downT[:, c, :], start=(c == 0), stop=(c == C - 1))
                last.then_inc(down_made, 1)

            turn_x(0)
            pe.wait_ge(w_ready, 4)
            project_q(0)
            project_k(0)
            pe.wait_ge(k_kept, 2)
            project_v()
            pe.wait_ge(v_kept, 1)
            turn_x(1)
            project_q(1)
            project_k(1)
            for ahead in range(2):
                wait_stack(0, ahead)
                for t in range(NT):
                    for j in range(J):
                        score_a(0, ahead, t, j)
                if ahead == 0:
                    pe.wait_ge(k_kept, 4)
                    turn_shift(0, 0)

            def misc(i, slot):
                post, v_ahead, proj = whole(i)
                if slot == 1 and v_ahead:
                    pe.wait_ge(shift_split, 2 * (G * i + 1) + 2)
                    project_v()
                if slot == 2 and proj:
                    pe.wait_ge(v_kept, i + 2)
                    turn_x(i + 2)
                if slot == 3 and proj:
                    project_q(i + 2)
                if slot == 4 and proj:
                    pe.wait_ge(shift_split, 2 * (G * i + 2) + 2)
                    project_k(i + 2)
                if slot == 5 and post:
                    pe.wait_ge(shift_split, 2 * (G * i + 2) + 2)
                    if proj:
                        pe.wait_ge(k_kept, 2 * (i + 2) + 2)
                    project_out(i - 1)
                if slot == 7 and post:
                    turn_x1(i - 1)
                if 8 <= slot <= 13 and post:
                    c, half = (slot - 8) // 2, slot % 2
                    if slot in (8, 12) and exists(i, slot // NT + 1):
                        pe.wait_ge(shift_split, 2 * (G * i + slot // NT + 1) + 2)
                    (up if half else gate)(i - 1, c)
                if slot == 14 and post:
                    down(i - 1)

            def free_for_shift(i, g):
                post, v_ahead, proj = whole(i)
                if g == 0:
                    if not isinstance(i, int):
                        pe.wait_ge(y2_made, i - 1)
                        pe.wait_ge(shift_split, 2 * (G * i))
                    elif i == 0:
                        pe.wait_ge(shift_split, 2)
                    else:
                        if i > 1:
                            pe.wait_ge(y2_made, i - 1)
                        pe.wait_ge(shift_split, 2 * (G * i))
                elif g == 1:
                    if proj:
                        pe.wait_ge(q_kept, 2 * (i + 2) + 2)
                    elif v_ahead:
                        pe.wait_ge(v_kept, i + 2)
                    else:
                        pe.wait_ge(shift_split, 2 * (G * i + 1) + 2)
                elif g == 2:
                    if post:
                        pe.wait_ge(x1T_kept, i)
                    else:
                        pe.wait_ge(k_kept, 2 * (i + 2) + 2)
                elif post:
                    pe.wait_ge(hidden_done, C * (i - 1) + 2)
                else:
                    pe.wait_ge(shift_split, 2 * (G * i + 3) + 2)

            def batch_round(i):
                for slot in range(G * NT):
                    g, t = slot // NT, slot % NT
                    ahead = g + 2
                    if t == 0:
                        pe.wait_ge(shift_filled[g], 32 * i + 32)
                    s = 16 * i + slot
                    if not isinstance(s, int) or s >= 1:
                        pe.wait_ge(exp_done, 2 * s - 1)
                    score_b(g, t, 0)
                    if exists(i, ahead):
                        if t == 0:
                            wait_stack(i, ahead)
                        score_a(i, ahead, t, 0)
                        score_a(i, ahead, t, 1)
                    if t == 0 and exists(i, g + 1):
                        free_for_shift(i, g)
                        turn_shift(i, g + 1)
                    if slot > 0:
                        weigh_values(i, slot - 1)
                    elif not isinstance(i, int) or i > 0:
                        weigh_values(i - 1, G * NT - 1)
                    score_b(g, t, 1)
                    if exists(i, ahead):
                        score_a(i, ahead, t, 2)
                        score_a(i, ahead, t, 3)
                    misc(i, slot)

            rounds(pe, batch_round)
            weigh_values(LAST, G * NT - 1)
            pe.wait_ge(y2_made, LAST)
            project_out(LAST)
            turn_x1(LAST)
            for c in range(C):
                gate(LAST, c)
                up(LAST, c)
            down(LAST)

        @block.scalar
        def _(act):
            act.wait_ge(bias_loaded, 48)
            act.mul(bias_q[:, :], bias_col[:, 0:1], 1.0 / SCALING).then_inc(bias_q_made, 1)
            for w, dst in enumerate((wT[:, :, :].rearrange("p c n -> p (c n)"), gateT[:, :], upT[:, :],
                                     downT[:, :, :].rearrange("p c n -> p (c n)"))):
                act.wait_ge(w_transposed, w + 1)
                act.copy(dst, ps_b[:, w, 0:dst.shape[-1]]).then_inc(w_ready, 1)
            act.wait_ge(bias_q_made, 1)

            def keep_xT(n):
                act.wait_ge(xT_made, n + 1)
                if not isinstance(n, int) or n >= 1:
                    act.wait_ge(v_made, n)
                act.copy(xT[:, :], ps_m[:, :]).then_inc(xT_kept, 1)

            def keep_q(n):
                act.wait_ge(q_made, n + 1)
                if not isinstance(n, int) or n >= 1:
                    act.wait_ge(q_stored, 48 * n)
                act.activation(q_full[:, :], ps_m[:, :], ACT.Identity, bias=bias_q[:, :], scale=1.0 / SCALING
                               ).then_inc(q_kept, 1)
                act.activation(q_parts[:, 0, :], ps_m[:, :], ACT.Identity, bias=bias_q[:, :], scale=1.0 / SCALING
                               ).then_inc(q_kept, 1)

            def keep_k(n):
                act.wait_ge(k_made, n + 1)
                if not isinstance(n, int) or n >= 1:
                    act.wait_ge(k_stored, 48 * n)
                act.activation(k_full[:, :], ps_m[:, :], ACT.Identity, bias=bias_col[:, 1:2]).then_inc(k_kept, 1)
                act.activation(k_parts[:, 0, :], ps_m[:, :], ACT.Identity, bias=bias_col[:, 1:2]
                               ).then_inc(k_kept, 1)

            def keep_v(n):
                act.wait_ge(v_made, n + 1)
                if not isinstance(n, int) or n >= 1:
                    act.wait_ge(v_filled, G * n)
                act.copy(v_rows[:, :, :].rearrange("p t n -> p (t n)"), ps_m[:, :]).then_inc(v_kept, 1)

            def exponentials(i, slot, r):
                s = 16 * i + slot
                act.wait_ge(b_scored, 2 * s + r + 1)
                if r == 0 and (not isinstance(s, int) or s >= 2):
                    act.wait_ge(pv_done, s - 1)
                act.activation(probs[:, slot % 2, 2 * r:2 * r + 2, :], ps_b[:, 2 * r:2 * r + 2, :], ACT.Exp
                               ).then_inc(exp_done, 1)

            def keep_o(i, g):
                act.wait_ge(pv_done, NT * (G * i + g) + NT)
                if not isinstance(i, int) or G * i + g >= 2:
                    act.wait_ge(o_stored[g % 2], 16 * (2 * i + g // 2))
                act.copy(o_raw[:, g % 2, :], ps_o[:, :]).then_inc(o_kept, 1)

            def keep_x1T(n):
                act.wait_ge(x1T_made, n + 1)
                act.copy(x1T[:, :], ps_m[:, :]).then_inc(x1T_kept, 1)

            def gate_tanh(n, c):
                act.wait_ge(gate_made, C * n + c + 1)
                if not isinstance(n, int) or C * n + c >= 1:
                    act.wait_ge(gated_done, C * n + c)
                act.activation(tanh[:, :], ps_m[:, :], ACT.Tanh, scale=0.5).then_inc(tanh_done, 1)

            for n in range(2):
                keep_xT(n)
                keep_q(n)
                keep_k(n)
                if n == 0:
                    keep_v(n)

            def batch_round(i):
                post, v_ahead, proj = whole(i)
                for slot in range(G * NT):
                    g, t = slot // NT, slot % NT
                    if v_ahead and slot == 2:
                        keep_v(i + 1)
                    if proj and slot == 3:
                        keep_xT(i + 2)
                    if proj and slot == 4:
                        keep_q(i + 2)
                    if proj and slot == 5:
                        keep_k(i + 2)
                    if post and slot == 8:
                        keep_x1T(i - 1)
                    if post and slot in (9, 11, 13):
                        gate_tanh(i - 1, (slot - 9) // 2)
                    exponentials(i, slot, 0)
                    if t == 0 and g > 0:
                        keep_o(i, g - 1)
                    elif t == 0 and (not isinstance(i, int) or i > 0):
                        keep_o(i - 1, G - 1)
                    exponentials(i, slot, 1)

            rounds(act, batch_round)
            keep_o(LAST, G - 1)
            keep_x1T(LAST)
            for c in range(C):
                gate_tanh(LAST, c)

        @block.vector
        def _(dve):
            dve.memset(q_stack[:, :, :, :], 0.0).then_inc(stacks_zero, 1)
            dve.memset(k_stack[0:96, :, :, :], 0.0).then_inc(stacks_zero, 1)
            dve.memset(k_stack[96:128, :, :, :], 1.0).then_inc(stacks_zero, 1)
            dve.wait_ge(w_loaded, 80)
            for w, scale in enumerate((WEIGHT_SCALE, WEIGHT_SCALE, 0.5 * WEIGHT_SCALE)):
                dve.tensor_scalar(w_deq[:, w, :, :], w_int[:, w, :, :], scale, None, ALU.mult
                                  ).then_inc(w_scaled, 1)

            def maxima(i, ahead, t, j):
                a = 16 * (G * i + ahead) + 4 * t + j
                dve.wait_ge(a_scored, a + 1)
                dve.tensor_reduce(neg_max[:, ahead % 2, NT * j + t:NT * j + t + 1], ps_a[:, j % 2, :], AX.X,
                                  ALU.max, negate=True).then_inc(a_reduced, 1)

            def split_shift(i, ahead):
                u = G * i + ahead
                dve.wait_ge(shift_turned, u + 1)
                if not isinstance(i, int) or u >= 1:
                    n, g = (i, ahead - 1) if ahead % G else (i + ahead // G - 1, G - 1)
                    n = n + 0 if ahead % G == 0 else i + (ahead - 1) // G
                    dve.wait_ge(shift_filled[g % G], 32 * n + 32)
                dve.tensor_copy(shift_parts[:, 0, :], ps_m[0:J * NT, 0:P]).then_inc(shift_split, 1)
                dve.wait_ge(shift_split, 2 * u + 1)
                dve.tensor_tensor(shift_parts[:, 1, :], ps_m[0:J * NT, 0:P], shift_parts[:, 0, :],
                                  ALU.subtract).then_inc(shift_split, 1)

            def reciprocals(n):
                dve.wait_ge(o_loaded, 32 * n + 32)
                if not isinstance(n, int) or n >= 1:
                    dve.wait_ge(recip_stored, 16 * n)
                dve.reciprocal(recips[:, :], sums[:, :]).then_inc(recip_done, 1)

            def moments(n, y, made, done):
                dve.wait_ge(made, n + 1)
                for t in range(NT):
                    last = dve.bn_stats(stats[:, t, :], y[:, t, :])
                last.then_inc(done, 1)

            def aggregate(aggregated):
                for t in range(NT):
                    last = dve.bn_aggr(mean_var[:, t, :], stats[:, t, :])
                last.then_inc(aggregated, 1)

            def normalize(n, dst, y, ready, done):
                dve.wait_ge(ready, n + 1)
                for t in range(NT):
                    last = dve.tensor_scalar(dst[:, t, :], y[:, t, :], mean_var[:, t, 0:1], rstd[:, t:t + 1],
                                             ALU.subtract, ALU.mult)
                last.then_inc(done, 1)

            def residual_1(n):
                dve.wait_ge(out_made, n + 1)
                dve.wait_ge(x_bias_added, n + 1)
                dve.tensor_tensor(y1[:, :, :], ps_m[:, :].rearrange("p (t n) -> p t n", t=NT),
                                  x_biased[:, :, :], ALU.add).then_inc(y1_made, 1)

            def gate_product(n, c):
                dve.wait_ge(tanh_done, C * n + c + 1)
                dve.scalar_tensor_tensor(out=gated[:, :], in0=tanh[:, :], scalar=1.0, in1=ps_m[:, :],
                                         op0=ALU.add, op1=ALU.mult).then_inc(gated_done, 1)

            def up_product(n, c):
                dve.wait_ge(up_made, C * n + c + 1)
                dve.wait_ge(gated_done, C * n + c + 1)
                if c == 0 and (not isinstance(n, int) or n >= 1):
                    dve.wait_ge(down_made, n)
                dve.tensor_tensor(hidden[:, c, :], gated[:, :], ps_m[:, :], ALU.mult).then_inc(hidden_done, 1)

            def residual_2(n):
                dve.wait_ge(down_made, n + 1)
                dve.tensor_tensor(y2[:, :, :], ps_m[:, :].rearrange("p (t n) -> p t n", t=NT), x1[:, :, :],
                                  ALU.add).then_inc(y2_made, 1)

            def finish_rows(n):
                if not isinstance(n, int) or n >= 1:
                    dve.wait_ge(result_stored, 16 * n)
                normalize(n, result, y2, rstd2_ready, result_made)

            for ahead in range(2):
                for t in range(NT):
                    for j in range(J):
                        maxima(0, ahead, t, j)
                if ahead == 0:
                    split_shift(0, 0)

            def batch_round(i):
                post, v_ahead, proj = whole(i)
                for slot in range(G * NT):
                    g, t = slot // NT, slot % NT
                    ahead = g + 2
                    if slot == 3 and post:
                        reciprocals(i - 1)
                    if slot == 6 and post:
                        residual_1(i - 1)
                        moments(i - 1, y1, y1_made, y1_stats)
                    if slot == 7 and post:
                        normalize(i - 1, x1, y1, rstd1_ready, x1_made)
                    if slot in (10, 12, 14) and post:
                        up_product(i - 1, (slot - 10) // 2)
                    if slot == 15 and post:
                        residual_2(i - 1)
                        moments(i - 1, y2, y2_made, y2_stats)
                    if slot == 6 and post:
                        dve.wait_ge(y1_stats, i)
                    if slot == 15 and post:
                        dve.wait_ge(y2_stats, i)
                    if exists(i, ahead):
                        maxima(i, ahead, t, 0)
                    if slot == 6 and post:
                        aggregate(y1_mv)
                    if slot == 15 and post:
                        aggregate(y2_mv)
                    if exists(i, ahead):
                        maxima(i, ahead, t, 1)
                    if t == 0 and exists(i, g + 1):
                        split_shift(i, g + 1)
                    if slot in (9, 11, 13) and post:
                        gate_product(i - 1, (slot - 9) // 2)
                    if exists(i, ahead):
                        maxima(i, ahead, t, 2)
                        maxima(i, ahead, t, 3)
                if post:
                    finish_rows(i - 1)

            rounds(dve, batch_round)
            reciprocals(LAST)
            residual_1(LAST)
            moments(LAST, y1, y1_made, y1_stats)
            dve.wait_ge(y1_stats, B)
            aggregate(y1_mv)
            normalize(LAST, x1, y1, rstd1_ready, x1_made)
            for c in range(C):
                gate_product(LAST, c)
                up_product(LAST, c)
            residual_2(LAST)
            moments(LAST, y2, y2_made, y2_stats)
            dve.wait_ge(y2_stats, B)
            aggregate(y2_mv)
            finish_rows(LAST)

        @block.gpsimd
        def _(pool):
            pool.memset(ident[:, :], 0.0).then_inc(ident_zero, 1)
            pool.wait_ge(ident_zero, 1)
            pool.affine_select(out=ident[:, :], in_=ident[:, :], compare_op=ALU.not_equal, fill=1.0, base=0,
                               pattern=[[-1, P]], channel_multiplier=1).then_inc(ident_made, 1)
            pool.memset(v_ones[:, :, :, :, :], 1.0).then_inc(const_made, 1)
            pool.memset(minus_half[:, :], -0.5).then_inc(const_made, 1)
            pool.memset(eps[:, :], EPS).then_inc(const_made, 1)
            pool.memset(one[:, :], 1.0).then_inc(const_made, 1)
            pool.wait_ge(const_made, 4)
            pool.wait_ge(bias_loaded, 48)

            def split_parts(n, full, rest, parts, kept, chain):
                pool.wait_ge(kept, 2 * n + 2)
                pool.tensor_tensor(rest[:, :], full[:, :], parts[:, 0, :], ALU.subtract).then_inc(chain, 1)
                pool.wait_ge(chain, 3 * n + 1)
                pool.tensor_tensor(parts[:, 1, :], rest[:, :], one[:, :].to_broadcast([P, S]), ALU.mult
                                   ).then_inc(chain, 1)
                pool.wait_ge(chain, 3 * n + 2)
                pool.tensor_tensor(parts[:, 2, :], rest[:, :], parts[:, 1, :], ALU.subtract).then_inc(chain, 1)

            def lay_values(i, ahead):
                g = ahead % G
                cols = slice(J * HD * g, J * HD * (g + 1))
                pool.wait_ge(v_kept, i + ahead // G + 1)
                pool.tensor_tensor(v_ones[:, g, :, :, 0:HD],
                                   v_rows[:, :, cols].rearrange("p t (j d) -> p t j d", j=J),
                                   v_bias[:, cols].rearrange("p (o j d) -> p o j d", o=1, j=J)
                                   .to_broadcast([P, NT, J, HD]), ALU.add).then_inc(v_filled, 1)

            def add_out_bias(n):
                pool.wait_ge(x_reloaded, 16 * n + 16)
                if not isinstance(n, int) or n >= 1:
                    pool.wait_ge(y1_made, n)
                pool.tensor_tensor(x_biased[:, :, :], x_again[:, :, :],
                                   o_bias[:, :].rearrange("p (o n) -> p o n", o=1).to_broadcast([P, NT, P]),
                                   ALU.add).then_inc(x_bias_added, 1)

            def divide_o(n):
                pool.wait_ge(recip_loaded, 16 * n + 16)
                pool.wait_ge(o_loaded, 32 * n + 32)
                if not isinstance(n, int) or n >= 1:
                    pool.wait_ge(out_made, n)
                pool.tensor_tensor(oT_norm[:, :], oT[:, :], recip_rows[:, :], ALU.mult).then_inc(o_normed, 1)

            def inverse_deviation(n, aggregated, var_ready, ready):
                pool.wait_ge(aggregated, n + 1)
                pool.tensor_tensor(var_eps[:, :], mean_var[:, :, 1], eps[:, :], ALU.add).then_inc(var_ready, 1)
                pool.wait_ge(var_ready, n + 1)
                pool.tensor_tensor(rstd[:, :], var_eps[:, :], minus_half[:, :], ALU.pow).then_inc(ready, 1)

            split_parts(0, q_full, q_rest, q_parts, q_kept, q_chain)
            split_parts(0, k_full, k_rest, k_parts, k_kept, k_chain)
            for ahead in range(3):
                lay_values(0, ahead)
            split_parts(1, q_full, q_rest, q_parts, q_kept, q_chain)
            split_parts(1, k_full, k_rest, k_parts, k_kept, k_chain)

            def batch_round(i):
                post, v_ahead, proj = whole(i)
                for g in range(G):
                    if exists(i, g + 3):
                        if not (isinstance(i, int) and i == 0 and g == 0):
                            pool.wait_ge(pv_done, NT * (G * i + g))
                        lay_values(i, g + 3)
                    if g == 0 and post:
                        add_out_bias(i - 1)
                    if g == 1:
                        if proj:
                            split_parts(i + 2, q_full, q_rest, q_parts, q_kept, q_chain)
                        if post:
                            divide_o(i - 1)
                            inverse_deviation(i - 1, y1_mv, var1_ready, rstd1_ready)
                    if g == 2 and proj:
                        split_parts(i + 2, k_full, k_rest, k_parts, k_kept, k_chain)
                if post:
                    inverse_deviation(i - 1, y2_mv, var2_ready, rstd2_ready)

            rounds(pool, batch_round)
            add_out_bias(LAST)
            divide_o(LAST)
            inverse_deviation(LAST, y1_mv, var1_ready, rstd1_ready)
            inverse_deviation(LAST, y2_mv, var2_ready, rstd2_ready)


_INS = ['L0_attn_q', 'L0_attn_in_w', 'L0_attn_qkv_bias', 'L0_attn_out_w', 'L0_attn_out_b',
        'L0_ffn_w_gate', 'L0_ffn_w_up', 'L0_ffn_w_down']


def kernel(**inputs):
    import numpy as _np
    import concourse.bacc as _bacc
    from concourse import mybir as _mybir
    from concourse.bass_utils import run_bass_kernel_spmd as _run

    nc = _bacc.Bacc("TRN2", target_bir_lowering=False, num_devices=1)
    arrays, args = {}, []
    for name in _INS:
        a = _np.ascontiguousarray(inputs[name])
        arrays[f"in_{name}_dram"] = a
        args.append(nc.dram_tensor(f"in_{name}_dram", a.shape, _mybir.dt.from_np(a.dtype), kind="ExternalInput").ap())
    shape = inputs['L0_attn_q'].shape
    out = nc.dram_tensor("out_0_dram", shape, _mybir.dt.from_np(_np.dtype('float32')), kind="ExternalOutput").ap()
    transformer_layer(nc, *args, out)
    r = _run(nc, [arrays], core_ids=[0])
    return r.results[0]["out_0_dram"]
```

```python
from contextlib import ExitStack

import numpy as np

import concourse.bass as bass
from concourse import mybir

ALU = mybir.AluOpType
ACT = mybir.ActivationFunctionType
AX = mybir.AxisListType
F32 = mybir.dt.float32
BF16 = mybir.dt.bfloat16
I32 = mybir.dt.int32

P = 128
H = 16
HD = 8
G = 4
J = H // G
NT = 4
EPS = 1e-5
WEIGHT_SCALE = 1.0 / 127.0
PRODUCTS = 6
ROWS = HD * PRODUCTS
SHIFT_ROW = 96
SCORE_ROWS = 96
BANKS = 3
OROWS = 32


TWO_ONES = float(np.uint32(0x3F803F80).view(np.float32))


def transformer_layer(nc, x, in_w, qkv_bias, out_w, out_b, w_gate, w_up, w_down, out):
    B, S, D = x.shape
    HID = w_gate.shape[0]
    C = HID // P
    assert D == P and S == NT * P and HID == C * P and D == H * HD
    SCALING = float(HD) ** 0.5

    q_scratch = nc.dram_tensor("q_scratch", (B, P, PRODUCTS, S), BF16, kind="Internal").ap()
    k_scratch = nc.dram_tensor("k_scratch", (B, P, PRODUCTS, S), BF16, kind="Internal").ap()
    o_scratch = nc.dram_tensor("o_scratch", (B, H, OROWS, S), F32, kind="Internal").ap()
    r_scratch = nc.dram_tensor("r_scratch", (B, H, S), F32, kind="Internal").ap()

    x_rows = x.rearrange("b (t p) d -> b p t d", p=P)
    out_rows = out.rearrange("b (t p) d -> b p t d", p=P)
    q_stacks = q_scratch.rearrange("b (g j d) c s -> b g (d c) j s", g=G, j=J)
    k_stacks = k_scratch.rearrange("b (g j d) c s -> b g (d c) j s", g=G, j=J)

    with ExitStack() as ctx:
        def sb(name, shape, dt=F32):
            return ctx.enter_context(nc.sbuf_tensor(name, shape, dt))

        def psum(name, shape):
            return ctx.enter_context(nc.psum_tensor(name, shape, F32))

        def sem(name):
            return ctx.enter_context(nc.semaphore(name))

        ident = sb("ident", [P, P])
        in_w_sb = sb("in_w_sb", [P, 3, P])
        out_w_sb = sb("out_w_sb", [P, P])
        w_int = sb("w_int", [P, 3, C, P], I32)
        w_deq = sb("w_deq", [P, 3, C, P])
        wT = sb("wT", [P, 4, P])
        gateT = sb("gateT", [P, C * P])
        upT = sb("upT", [P, C * P])
        downT = sb("downT", [P, C, P])
        bias_col = sb("bias_col", [P, 3])
        bias_q = sb("bias_q", [P, 1])
        v_bias = sb("v_bias", [P, P])
        o_bias = sb("o_bias", [P, P])
        minus_half = sb("minus_half", [P, NT])
        eps = sb("eps", [P, NT])
        one = sb("one", [P, 1])
        x_in = sb("x_in", [P, NT, P])
        xT = sb("xT", [P, S])
        q_full = sb("q_full", [P, S])
        k_full = sb("k_full", [P, S])
        q_rest = sb("q_rest", [P, S])
        k_rest = sb("k_rest", [P, S])
        q_parts = sb("q_parts", [P, 3, S], BF16)
        k_parts = sb("k_parts", [P, 3, S], BF16)
        v_rows = sb("v_rows", [P, NT, P])
        q_stack = sb("q_stack", [P, G, J, S], BF16)
        k_stack = sb("k_stack", [P, G, J, S], BF16)
        v_ones = sb("v_ones", [P, G, NT, J, OROWS])
        neg_max = sb("neg_max", [P, 2, J * NT])
        shift_parts = sb("shift_parts", [J * NT, 2, P], BF16)
        probs = sb("probs", [P, 2, J, S])
        o_raw = sb("o_raw", [P, 2, S])
        oT = sb("oT", [P, S])
        sums = sb("sums", [P, H * S // P])
        recips = sb("recips", [P, H * S // P])
        recip_rows = sb("recip_rows", [P, S])
        oT_norm = sb("oT_norm", [P, S])
        x_again = sb("x_again", [P, NT, P])
        x_biased = sb("x_biased", [P, NT, P])
        y1 = sb("y1", [P, NT, P])
        y2 = sb("y2", [P, NT, P])
        stats = sb("stats", [P, NT, 6])
        mean_var = sb("mean_var", [P, NT, 2])
        var_eps = sb("var_eps", [P, NT])
        rstd = sb("rstd", [P, NT])
        x1 = sb("x1", [P, NT, P])
        x1T = sb("x1T", [P, S])
        tanh = sb("tanh", [P, S])
        gated = sb("gated", [P, S])
        up_rows = sb("up_rows", [P, S])
        hidden = sb("hidden", [P, C, S])
        result = sb("result", [P, NT, P])

        ps_b = psum("ps_b", [P, BANKS, S])
        ps_a = psum("ps_a", [P, BANKS, S])
        ps_o = psum("ps_o", [P, S])
        ps_m = psum("ps_m", [P, S])

        w_loaded = sem("w_loaded")
        bias_loaded = sem("bias_loaded")
        x_loaded = sem("x_loaded")
        ident_zero = sem("ident_zero")
        ident_made = sem("ident_made")
        stacks_zero = sem("stacks_zero")
        const_made = sem("const_made")
        bias_q_made = sem("bias_q_made")
        w_scaled = sem("w_scaled")
        w_transposed = sem("w_transposed")
        w_ready = sem("w_ready")
        ffn_w_loaded = sem("ffn_w_loaded")
        xT_made = sem("xT_made")
        xT_kept = sem("xT_kept")
        q_made = sem("q_made")
        k_made = sem("k_made")
        q_kept = sem("q_kept")
        k_kept = sem("k_kept")
        q_chain = sem("q_chain")
        k_chain = sem("k_chain")
        v_made = sem("v_made")
        v_kept = sem("v_kept")
        v_filled = sem("v_filled")
        q_stored = sem("q_stored")
        k_stored = sem("k_stored")
        stack_filled = [sem(f"stack_filled{g}") for g in range(G)]
        shift_filled = [sem(f"shift_filled{g}") for g in range(G)]
        a_scored = sem("a_scored")
        a_reduced = sem("a_reduced")
        shift_turned = sem("shift_turned")
        shift_split = sem("shift_split")
        b_scored = sem("b_scored")
        exp_done = sem("exp_done")
        pv_done = sem("pv_done")
        o_kept = sem("o_kept")
        o_stored = [sem(f"o_stored{n}") for n in range(2)]
        o_loaded = sem("o_loaded")
        recip_done = sem("recip_done")
        recip_stored = sem("recip_stored")
        recip_loaded = sem("recip_loaded")
        o_normed = sem("o_normed")
        x_reloaded = sem("x_reloaded")
        x_bias_added = sem("x_bias_added")
        out_made = sem("out_made")
        y1_made = sem("y1_made")
        y1_stats = sem("y1_stats")
        y1_mv = sem("y1_mv")
        var1_ready = sem("var1_ready")
        rstd1_ready = sem("rstd1_ready")
        x1_made = sem("x1_made")
        x1T_made = sem("x1T_made")
        x1T_kept = sem("x1T_kept")
        gate_made = sem("gate_made")
        tanh_done = sem("tanh_done")
        gated_done = sem("gated_done")
        up_made = sem("up_made")
        up_kept = sem("up_kept")
        hidden_done = sem("hidden_done")
        down_made = sem("down_made")
        y2_made = sem("y2_made")
        y2_stats = sem("y2_stats")
        y2_mv = sem("y2_mv")
        var2_ready = sem("var2_ready")
        rstd2_ready = sem("rstd2_ready")
        result_made = sem("result_made")
        result_stored = sem("result_stored")

        LAST = B - 1

        def whole(i):
            known = isinstance(i, int)
            rest = not known or i >= 2
            post = not known or i >= 1
            v_ahead = not known or i + 1 <= LAST
            proj = not known or i + 2 <= LAST
            return rest, post, v_ahead, proj

        def since(tile, before):
            if tile >= BANKS or before == 0:
                return BANKS
            return min(n for n in range(tile + 1, tile + before + 1) if (before + tile - n) % BANKS == tile % BANKS)

        def exists(i, unit_ahead):
            return not isinstance(i, int) or G * i + unit_ahead < G * B

        def rounds(eng, batch_round):
            batch_round(0)
            batch_round(1)
            with eng.Fori(2, B - 2) as i:
                batch_round(i)
            batch_round(B - 2)
            batch_round(B - 1)

        block = ctx.enter_context(nc.Block())

        @block.sync
        def _(sp):
            sp.dma_start(x_in[:, :, :], x_rows[0]).then_inc(x_loaded, 16)
            sp.dma_start(in_w_sb[:, :, :], in_w.rearrange("(c p) d -> p c d", p=P)).then_inc(w_loaded, 16)
            sp.dma_start(out_w_sb[:, :], out_w).then_inc(w_loaded, 16)
            sp.dma_start(w_int[:, 0, :, :], w_gate.rearrange("(c p) d -> p c d", p=P)).then_inc(ffn_w_loaded, 16)
            sp.dma_start(w_int[:, 1, :, :], w_up.rearrange("(c p) d -> p c d", p=P)).then_inc(ffn_w_loaded, 16)
            sp.dma_start(w_int[:, 2, :, :], w_down.rearrange("p (c n) -> p c n", c=C)).then_inc(ffn_w_loaded, 16)

            def load_x(n):
                sp.wait_ge(xT_made, n)
                sp.dma_start(x_in[:, :, :], x_rows[n]).then_inc(x_loaded, 16)

            def store_q(n):
                sp.wait_ge(q_chain, 3 * n + 3)
                sp.dma_start(q_scratch[n, :, 0:3, :], q_parts[:, 0:3, :]).then_inc(q_stored, 16)
                sp.dma_start(q_scratch[n, :, 3:5, :], q_parts[:, 0:2, :]).then_inc(q_stored, 16)
                sp.dma_start(q_scratch[n, :, 5:6, :], q_parts[:, 0:1, :]).then_inc(q_stored, 16)

            def store_k(n):
                sp.wait_ge(k_chain, 3 * n + 3)
                sp.dma_start(k_scratch[n, :, 0:3, :], k_parts[:, 0:1, :].to_broadcast([P, 3, S])
                             ).then_inc(k_stored, 16)
                sp.dma_start(k_scratch[n, :, 3:5, :], k_parts[:, 1:2, :].to_broadcast([P, 2, S])
                             ).then_inc(k_stored, 16)
                sp.dma_start(k_scratch[n, :, 5:6, :], k_parts[:, 2:3, :]).then_inc(k_stored, 16)

            def fill_stacks(i, ahead):
                n, g = i + ahead // G, ahead % G
                if g == 0 or isinstance(i, int):
                    sp.wait_ge(q_stored, 48 * n + 48)
                    sp.wait_ge(k_stored, 48 * n + 48)
                sp.dma_start(q_stack[0:ROWS, g, :, :], q_stacks[n, g]).then_inc(stack_filled[g], 16)
                sp.dma_start(k_stack[0:ROWS, g, :, :], k_stacks[n, g]).then_inc(stack_filled[g], 16)

            def fill_shift(i, ahead):
                g = ahead % G
                sp.wait_ge(shift_split, 2 * (G * i + ahead) + 2)
                for c in range(2):
                    row = q_stack[SHIFT_ROW + c:SHIFT_ROW + c + 1, g, :, :].rearrange("o j s -> o (j s)")
                    sp.dma_start(row, shift_parts[:, c, :]).then_inc(shift_filled[g], 16)

            def store_o(i, behind):
                g = G - behind
                sp.wait_ge(o_kept, G * i + g + 1)
                sp.dma_start(o_scratch[i, J * g:J * g + J].rearrange("j r s -> (j r) s"), o_raw[:, g % 2, :]
                             ).then_inc(o_stored[g % 2], 16)

            def normalizer(n):
                sp.wait_ge(o_stored[0], 32 * n + 32)
                sp.wait_ge(o_stored[1], 32 * n + 32)
                sp.dma_start(sums[:, :], o_scratch[n, :, HD, :].rearrange("h (c w) -> h c w", c=P // H)
                             ).then_inc(o_loaded, 16)
                sp.dma_start(oT[:, :], o_scratch[n, :, 0:HD, :]).then_inc(o_loaded, 16)
                sp.wait_ge(recip_done, n + 1)
                sp.dma_start(r_scratch[n].rearrange("h (c w) -> (h c) w", c=P // H), recips[:, :]
                             ).then_inc(recip_stored, 16)
                sp.wait_ge(recip_stored, 16 * n + 16)
                sp.dma_start(recip_rows[:, :],
                             r_scratch[n].rearrange("h (o s) -> h o s", o=1).to_broadcast([H, HD, S])
                             ).then_inc(recip_loaded, 16)

            def reload_x(n):
                if not isinstance(n, int) or n >= 1:
                    sp.wait_ge(x_bias_added, n)
                sp.dma_start(x_again[:, :, :], x_rows[n]).then_inc(x_reloaded, 16)

            def store_result(n):
                sp.wait_ge(result_made, n + 1)
                sp.dma_start(out_rows[n], result[:, :, :]).then_inc(result_stored, 16)

            load_x(1)
            store_q(0)
            store_k(0)
            sp.wait_ge(stacks_zero, 3)
            for ahead in range(2):
                fill_stacks(0, ahead)
            fill_stacks(0, 2)
            fill_shift(0, 0)
            store_q(1)
            store_k(1)

            def batch_round(i):
                rest, post, v_ahead, proj = whole(i)
                for g in range(G):
                    if exists(i, g + 3):
                        if not (isinstance(i, int) and i == 0 and g == 0):
                            sp.wait_ge(b_scored, 16 * (G * i + g))
                        fill_stacks(i, g + 3)
                    if g == 0 and proj:
                        load_x(i + 2)
                    if exists(i, g + 1):
                        fill_shift(i, g + 1)
                    if g > 0:
                        store_o(i, G - g + 1)
                    elif post:
                        store_o(i - 1, 1)
                    if g == 0 and post:
                        reload_x(i - 1)
                        normalizer(i - 1)
                    if g == 1 and rest:
                        store_result(i - 2)
                    if g == 2 and proj:
                        store_q(i + 2)
                    if g == 3 and proj:
                        store_k(i + 2)

            rounds(sp, batch_round)
            store_o(LAST, 1)
            normalizer(LAST)
            reload_x(LAST)
            store_result(LAST - 1)
            for half in range(2):
                ts = slice(2 * half, 2 * half + 2)
                sp.wait_ge(result_made, LAST + half + 1)
                sp.dma_start(out_rows[LAST, :, ts, :], result[:, ts, :]).then_inc(result_stored, 16)
            sp.wait_ge(result_stored, 16 * (B + 1))

        @block.tensor
        def _(pe):
            pe.wait_ge(ident_made, 1)

            def turn_ffn_weights():
                for w in range(3):
                    pe.wait_ge(w_scaled, w + 1)
                    for c in range(C):
                        last = pe.transpose(ps_b[:, w, c * P:(c + 1) * P], w_deq[:, w, c, :], ident[:, :])
                    last.then_inc(w_transposed, 1)

            def turn_x(n):
                pe.wait_ge(x_loaded, 16 * n + 16)
                for t in range(NT):
                    last = pe.transpose(ps_m[:, t * P:(t + 1) * P], x_in[:, t, :], ident[:, :])
                last.then_inc(xT_made, 1)

            def project_q(n):
                pe.wait_ge(xT_kept, n + 1)
                pe.matmul(ps_m[:, :], wT[:, 0, :], xT[:, :], start=True, stop=True).then_inc(q_made, 1)

            def project_k(n):
                pe.wait_ge(q_kept, 2 * n + 2)
                pe.matmul(ps_m[:, :], wT[:, 1, :], xT[:, :], start=True, stop=True).then_inc(k_made, 1)

            def project_v():
                for t in range(NT):
                    last = pe.matmul(ps_m[:, t * P:(t + 1) * P], xT[:, t * P:(t + 1) * P], wT[:, 2, :],
                                     start=True, stop=True)
                last.then_inc(v_made, 1)

            def score_a(i, ahead, t, j, tile, before):
                g = ahead % G
                a = 16 * (G * i + ahead) + 4 * t + j
                free = a - since(tile, before) + 1
                if not isinstance(free, int) or free > 0:
                    pe.wait_ge(a_reduced, free)
                pe.matmul(ps_a[:, tile % BANKS, :], q_stack[0:SCORE_ROWS, g, j, t * P:(t + 1) * P],
                          k_stack[0:SCORE_ROWS, g, j, :], start=True, stop=True).then_inc(a_scored, 1)

            def wait_stack(i, ahead):
                pe.wait_ge(stack_filled[ahead % G], 32 * (i + ahead // G) + 32)

            def score_b(i, g, t, j):
                tile = 4 * (NT * g + t) + j
                free = 64 * i + tile - since(tile, 64) + 1
                if not isinstance(free, int) or free > 0:
                    pe.wait_ge(exp_done, free)
                pe.matmul(ps_b[:, tile % BANKS, :], k_stack[:, g, j, t * P:(t + 1) * P], q_stack[:, g, j, :],
                          start=True, stop=True).then_inc(b_scored, 1)

            def weigh_values(i, slot):
                g, t = slot // NT, slot % NT
                pe.wait_ge(exp_done, 4 * (16 * i + slot) + 4)
                if t == 0:
                    pe.wait_ge(v_filled, G * i + g + 1)
                    if not isinstance(i, int) or G * i + g >= 1:
                        pe.wait_ge(o_kept, G * i + g)
                for j in range(J):
                    last = pe.matmul(ps_o[OROWS * j:OROWS * j + OROWS, :], v_ones[:, g, t, j, :],
                                     probs[:, t % 2, j, :], start=(t == 0), stop=(t == NT - 1))
                last.then_inc(pv_done, 1)

            def turn_shift(i, ahead):
                pe.wait_ge(a_reduced, 16 * (G * i + ahead) + 16)
                pe.transpose(ps_m[0:J * NT, 0:P], neg_max[:, ahead % 2, :], ident[:, :]).then_inc(shift_turned, 1)

            def project_out(n):
                pe.wait_ge(o_normed, n + 1)
                for t in range(NT):
                    last = pe.matmul(ps_m[:, t * P:(t + 1) * P], oT_norm[:, t * P:(t + 1) * P], wT[:, 3, :],
                                     start=True, stop=True)
                last.then_inc(out_made, 1)

            def turn_x1(n):
                pe.wait_ge(x1_made, n + 1)
                for t in range(NT):
                    last = pe.transpose(ps_m[:, t * P:(t + 1) * P], x1[:, t, :], ident[:, :])
                last.then_inc(x1T_made, 1)

            def gate(n, c, bank):
                pe.wait_ge(x1T_kept, n + 1)
                pe.matmul(bank, gateT[:, c * P:(c + 1) * P], x1T[:, :], start=True, stop=True
                          ).then_inc(gate_made, 1)

            def up(n, c, bank):
                pe.matmul(bank, upT[:, c * P:(c + 1) * P], x1T[:, :], start=True, stop=True
                          ).then_inc(up_made, 1)

            def down(n, half, bank):
                pe.wait_ge(hidden_done, C * n + C)
                for t in (2 * half, 2 * half + 1):
                    for c in range(C):
                        last = pe.matmul(bank[:, t * P:(t + 1) * P], hidden[:, c, t * P:(t + 1) * P],
                                         downT[:, c, :], start=(c == 0), stop=(c == C - 1))
                last.then_inc(down_made, 1)

            turn_x(0)
            pe.wait_ge(w_loaded, 32)
            for c in range(3):
                pe.transpose(ps_b[:, 0, c * P:(c + 1) * P], in_w_sb[:, c, :], ident[:, :])
            pe.transpose(ps_b[:, 0, 3 * P:4 * P], out_w_sb[:, :], ident[:, :]).then_inc(w_transposed, 1)
            pe.wait_ge(w_ready, 1)
            project_q(0)
            project_k(0)
            pe.wait_ge(k_kept, 2)
            project_v()
            turn_ffn_weights()
            pe.wait_ge(v_kept, 1)
            turn_x(1)
            project_q(1)
            project_k(1)
            for ahead in range(2):
                wait_stack(0, ahead)
                for t in range(NT):
                    for j in range(J):
                        score_a(0, ahead, t, j, 16 * ahead + 4 * t + j, 0)
                if ahead == 0:
                    pe.wait_ge(k_kept, 4)
                    turn_shift(0, 0)
            pe.wait_ge(w_ready, 4)

            def split_of(i, ahead):
                pe.wait_ge(shift_split, 2 * (G * i + ahead) + 2)

            def misc(i, slot):
                rest, post, v_ahead, proj = whole(i)
                n = i - 1
                if slot == 0 and rest:
                    split_of(i, 1)
                    down(i - 2, 0, ps_m)
                if slot == 1 and rest:
                    pe.wait_ge(y2_made, 2 * (i - 2) + 1)
                    down(i - 2, 1, ps_m)
                if slot == 2 and v_ahead:
                    if rest:
                        pe.wait_ge(y2_made, 2 * (i - 1))
                    else:
                        split_of(i, 1)
                    project_v()
                if slot == 3 and proj:
                    pe.wait_ge(v_kept, i + 2)
                    turn_x(i + 2)
                if slot == 4 and proj:
                    split_of(i, 2)
                    project_q(i + 2)
                if slot == 5 and post:
                    if proj:
                        pe.wait_ge(q_kept, 2 * (i + 2) + 2)
                    else:
                        split_of(i, 2)
                    project_out(n)
                if slot == 6 and proj:
                    if post:
                        pe.wait_ge(y1_made, i)
                    project_k(i + 2)
                if slot == 8 and post:
                    split_of(i, 3)
                    turn_x1(n)
                if slot == 9 and post:
                    gate(n, 0, ps_m[:, :])
                if slot == 10 and post:
                    pe.wait_ge(gated_done, C * n + 1)
                    up(n, 0, ps_m[:, :])
                if slot == 12 and post:
                    if exists(i, 4):
                        split_of(i, 4)
                    else:
                        pe.wait_ge(up_kept, C * n + 1)
                    gate(n, 1, ps_m[:, :])
                if slot == 13 and post:
                    pe.wait_ge(gated_done, C * n + 2)
                    up(n, 1, ps_m[:, :])
                if slot == 14 and post:
                    pe.wait_ge(up_kept, C * n + 2)
                    gate(n, 2, ps_m[:, :])
                if slot == 15 and post:
                    pe.wait_ge(gated_done, C * n + 3)
                    up(n, 2, ps_m[:, :])

            def free_for_shift(i, g):
                rest, post, v_ahead, proj = whole(i)
                if g == 0:
                    split_of(i, 0)
                    if rest:
                        pe.wait_ge(up_kept, C * (i - 2) + C)
                elif g == 1:
                    if proj:
                        pe.wait_ge(xT_kept, i + 3)
                    elif v_ahead:
                        pe.wait_ge(v_kept, i + 2)
                    else:
                        pe.wait_ge(y2_made, 2 * (i - 1))
                elif g == 2:
                    if proj:
                        pe.wait_ge(k_kept, 2 * (i + 2) + 2)
                    else:
                        pe.wait_ge(y1_made, i)
                elif post:
                    pe.wait_ge(up_kept, C * (i - 1) + 1)
                else:
                    split_of(i, 3)

            def batch_round(i):
                before = 2 * 16 if isinstance(i, int) and i == 0 else 64
                for slot in range(G * NT):
                    g, t = slot // NT, slot % NT
                    ahead = g + 2
                    if t == 0:
                        pe.wait_ge(shift_filled[g], 32 * i + 32)
                        if exists(i, ahead):
                            wait_stack(i, ahead)
                    for j in range(J):
                        if exists(i, ahead):
                            score_a(i, ahead, t, j, 4 * slot + j, before)
                        score_b(i, g, t, j)
                        if j == 1:
                            if slot > 0:
                                weigh_values(i, slot - 1)
                            elif not isinstance(i, int) or i > 0:
                                weigh_values(i - 1, G * NT - 1)
                            if t == 0 and exists(i, g + 1):
                                free_for_shift(i, g)
                                turn_shift(i, g + 1)
                    misc(i, slot)

            rounds(pe, batch_round)
            weigh_values(LAST, G * NT - 1)
            pe.wait_ge(up_kept, C * LAST)
            down(LAST - 1, 0, ps_m)
            pe.wait_ge(y2_made, 2 * (LAST - 1) + 1)
            down(LAST - 1, 1, ps_m)
            pe.wait_ge(y2_made, 2 * LAST)
            project_out(LAST)
            turn_x1(LAST)
            pe.wait_ge(exp_done, 64 * B)
            for c in range(C):
                gate(LAST, c, ps_b[:, c, :])
                up(LAST, c, ps_a[:, c, :])
            pe.wait_ge(o_kept, G * B)
            for half, bank in enumerate((ps_o, ps_m)):
                down(LAST, half, bank)

        @block.scalar
        def _(act):
            with nc.allow_non_contiguous_dma(reason="a bias per partition, 384 numbers once"):
                act.dma_start(bias_col[:, :], qkv_bias.rearrange("(c p) -> p c", p=P)).then_inc(bias_loaded, 16)
            bias_2d = qkv_bias.rearrange("(a n) -> a n", a=1)
            act.dma_start(v_bias[:, :], bias_2d[:, 2 * P:3 * P].to_broadcast([P, P])).then_inc(bias_loaded, 16)
            act.dma_start(o_bias[:, :], out_b.rearrange("(a n) -> a n", a=1).to_broadcast([P, P])
                          ).then_inc(bias_loaded, 16)

            def keep_weights(w, dst, src):
                act.wait_ge(w_transposed, w + 1)
                act.copy(dst, src).then_inc(w_ready, 1)

            def keep_xT(n):
                act.wait_ge(xT_made, n + 1)
                if not isinstance(n, int) or n >= 1:
                    act.wait_ge(v_made, n)
                act.copy(xT[:, :], ps_m[:, :]).then_inc(xT_kept, 1)

            def keep_q(n):
                act.wait_ge(q_made, n + 1)
                if not isinstance(n, int) or n >= 1:
                    act.wait_ge(q_stored, 48 * n)
                act.activation(q_full[:, :], ps_m[:, :], ACT.Identity, bias=bias_q[:, :], scale=1.0 / SCALING
                               ).then_inc(q_kept, 1)
                act.activation(q_parts[:, 0, :], ps_m[:, :], ACT.Identity, bias=bias_q[:, :], scale=1.0 / SCALING
                               ).then_inc(q_kept, 1)

            def keep_k(n):
                act.wait_ge(k_made, n + 1)
                if not isinstance(n, int) or n >= 1:
                    act.wait_ge(k_stored, 48 * n)
                act.activation(k_full[:, :], ps_m[:, :], ACT.Identity, bias=bias_col[:, 1:2]).then_inc(k_kept, 1)
                act.activation(k_parts[:, 0, :], ps_m[:, :], ACT.Identity, bias=bias_col[:, 1:2]
                               ).then_inc(k_kept, 1)

            def keep_v(n):
                act.wait_ge(v_made, n + 1)
                if not isinstance(n, int) or n >= 1:
                    act.wait_ge(v_filled, G * n)
                act.copy(v_rows[:, :, :].rearrange("p t n -> p (t n)"), ps_m[:, :]).then_inc(v_kept, 1)

            def exponentials(i, slot, j):
                s = 16 * i + slot
                act.wait_ge(b_scored, 4 * s + j + 1)
                if j == 0 and (not isinstance(s, int) or s >= 2):
                    act.wait_ge(pv_done, s - 1)
                act.activation(probs[:, slot % 2, j, :], ps_b[:, (4 * slot + j) % BANKS, :], ACT.Exp
                               ).then_inc(exp_done, 1)

            def keep_o(i, g):
                act.wait_ge(pv_done, NT * (G * i + g) + NT)
                if not isinstance(i, int) or G * i + g >= 2:
                    act.wait_ge(o_stored[g % 2], 16 * (2 * i + g // 2))
                act.copy(o_raw[:, g % 2, :], ps_o[:, :]).then_inc(o_kept, 1)

            def keep_x1T(n):
                act.wait_ge(x1T_made, n + 1)
                act.copy(x1T[:, :], ps_m[:, :]).then_inc(x1T_kept, 1)

            def gate_tanh(n, c):
                act.wait_ge(gate_made, C * n + c + 1)
                if not isinstance(n, int) or C * n + c >= 1:
                    act.wait_ge(gated_done, C * n + c)
                act.activation(tanh[:, :], ps_m[:, :], ACT.Tanh, scale=0.5).then_inc(tanh_done, 1)

            def keep_up(n, c):
                act.wait_ge(up_made, C * n + c + 1)
                if not isinstance(n, int) or C * n + c >= 1:
                    act.wait_ge(hidden_done, C * n + c)
                act.copy(up_rows[:, :], ps_m[:, :]).then_inc(up_kept, 1)

            keep_xT(0)
            keep_weights(0, wT[:, :, :].rearrange("p c n -> p (c n)"), ps_b[:, 0, :])
            act.wait_ge(bias_loaded, 48)
            act.mul(bias_q[:, :], bias_col[:, 0:1], 1.0 / SCALING).then_inc(bias_q_made, 1)
            act.wait_ge(bias_q_made, 1)
            keep_q(0)
            keep_k(0)
            keep_v(0)
            keep_weights(1, gateT[:, :], ps_b[:, 0, 0:C * P])
            keep_weights(2, upT[:, :], ps_b[:, 1, 0:C * P])
            keep_weights(3, downT[:, :, :].rearrange("p c n -> p (c n)"), ps_b[:, 2, 0:C * P])
            keep_xT(1)
            keep_q(1)
            keep_k(1)

            def batch_round(i):
                rest, post, v_ahead, proj = whole(i)
                for slot in range(G * NT):
                    g, t = slot // NT, slot % NT
                    exponentials(i, slot, 0)
                    if rest and slot == 0:
                        keep_up(i - 2, 2)
                    if v_ahead and slot == 3:
                        keep_v(i + 1)
                    if proj and slot == 4:
                        keep_xT(i + 2)
                    if proj and slot == 5:
                        keep_q(i + 2)
                    if proj and slot == 7:
                        keep_k(i + 2)
                    if post and slot == 9:
                        keep_x1T(i - 1)
                    if post and slot in (10, 13, 15):
                        gate_tanh(i - 1, (10, 13, 15).index(slot))
                    if post and slot in (11, 14):
                        keep_up(i - 1, (11, 14).index(slot))
                    exponentials(i, slot, 1)
                    exponentials(i, slot, 2)
                    if t == 0 and g > 0:
                        keep_o(i, g - 1)
                    elif t == 0 and (not isinstance(i, int) or i > 0):
                        keep_o(i - 1, G - 1)
                    exponentials(i, slot, 3)

            rounds(act, batch_round)
            keep_up(LAST - 1, 2)
            keep_o(LAST, G - 1)
            keep_x1T(LAST)
            for c in range(C):
                act.wait_ge(gate_made, C * LAST + c + 1)
                act.activation(probs[:, 0, c, :], ps_b[:, c, :], ACT.Tanh, scale=0.5).then_inc(tanh_done, 1)

        @block.vector
        def _(dve):
            words = [t[:, :, :, :].rearrange("p g j s -> p (g j s)").bitcast(F32) for t in (q_stack, k_stack)]
            dve.memset(words[0], 0.0).then_inc(stacks_zero, 1)
            dve.memset(words[1][96:128], TWO_ONES).then_inc(stacks_zero, 1)
            dve.wait_ge(ffn_w_loaded, 48)
            for w, scale in enumerate((WEIGHT_SCALE, WEIGHT_SCALE, 0.5 * WEIGHT_SCALE)):
                dve.tensor_scalar(w_deq[:, w, :, :], w_int[:, w, :, :], scale, None, ALU.mult
                                  ).then_inc(w_scaled, 1)

            def split_parts(n, full, rest, parts, kept, chain):
                dve.wait_ge(kept, 2 * n + 2)
                dve.tensor_tensor(rest[:, :], full[:, :], parts[:, 0, :], ALU.subtract).then_inc(chain, 1)
                dve.wait_ge(chain, 3 * n + 1)
                dve.tensor_copy(parts[:, 1, :], rest[:, :]).then_inc(chain, 1)
                dve.wait_ge(chain, 3 * n + 2)
                dve.tensor_tensor(parts[:, 2, :], rest[:, :], parts[:, 1, :], ALU.subtract).then_inc(chain, 1)

            def maxima(i, ahead, t, j, tile):
                a = 16 * (G * i + ahead) + 4 * t + j
                dve.wait_ge(a_scored, a + 1)
                dve.tensor_reduce(neg_max[:, ahead % 2, NT * j + t:NT * j + t + 1], ps_a[:, tile % BANKS, :],
                                  AX.X, ALU.max, negate=True).then_inc(a_reduced, 1)

            def split_shift(i, ahead):
                u = G * i + ahead
                dve.wait_ge(shift_turned, u + 1)
                if not isinstance(i, int) or u >= 1:
                    n, g = (i, ahead - 1) if ahead % G else (i + ahead // G - 1, G - 1)
                    n = n + 0 if ahead % G == 0 else i + (ahead - 1) // G
                    dve.wait_ge(shift_filled[g % G], 32 * n + 32)
                dve.tensor_copy(shift_parts[:, 0, :], ps_m[0:J * NT, 0:P]).then_inc(shift_split, 1)
                dve.wait_ge(shift_split, 2 * u + 1)
                dve.tensor_tensor(shift_parts[:, 1, :], ps_m[0:J * NT, 0:P], shift_parts[:, 0, :],
                                  ALU.subtract).then_inc(shift_split, 1)

            def reciprocals(n):
                dve.wait_ge(o_loaded, 32 * n + 32)
                if not isinstance(n, int) or n >= 1:
                    dve.wait_ge(recip_stored, 16 * n)
                dve.reciprocal(recips[:, :], sums[:, :]).then_inc(recip_done, 1)

            def moments(y, ts, done):
                for t in ts:
                    last = dve.bn_stats(stats[:, t, :], y[:, t, :])
                last.then_inc(done, 1)

            def aggregate(ts, aggregated):
                for t in ts:
                    last = dve.bn_aggr(mean_var[:, t, :], stats[:, t, :])
                last.then_inc(aggregated, 1)

            def normalize(dst, y, ts, done):
                for t in ts:
                    last = dve.tensor_scalar(dst[:, t, :], y[:, t, :], mean_var[:, t, 0:1], rstd[:, t:t + 1],
                                             ALU.subtract, ALU.mult)
                last.then_inc(done, 1)

            def residual_1(n):
                dve.wait_ge(out_made, n + 1)
                dve.wait_ge(x_bias_added, n + 1)
                dve.tensor_tensor(y1[:, :, :], ps_m[:, :].rearrange("p (t n) -> p t n", t=NT),
                                  x_biased[:, :, :], ALU.add).then_inc(y1_made, 1)

            def gate_product(n, c, t, bank, out):
                dve.wait_ge(tanh_done, C * n + c + 1)
                if not isinstance(n, int) or C * n + c >= 1:
                    dve.wait_ge(hidden_done, C * n + c)
                dve.scalar_tensor_tensor(out=out, in0=t, scalar=1.0, in1=bank, op0=ALU.add, op1=ALU.mult
                                         ).then_inc(gated_done, 1)

            def residual_2(n, half, bank):
                dve.wait_ge(down_made, 2 * n + half + 1)
                ts = slice(2 * half, 2 * half + 2)
                dve.tensor_tensor(y2[:, ts, :], bank[:, 2 * half * P:2 * (half + 1) * P]
                                  .rearrange("p (t n) -> p t n", t=2), x1[:, ts, :], ALU.add
                                  ).then_inc(y2_made, 1)

            def finish_rows(n):
                dve.wait_ge(rstd2_ready, n + 1)
                if not isinstance(n, int) or n >= 1:
                    dve.wait_ge(result_stored, 16 * n)
                normalize(result, y2, range(NT), result_made)

            for n in range(2):
                split_parts(n, q_full, q_rest, q_parts, q_kept, q_chain)
                split_parts(n, k_full, k_rest, k_parts, k_kept, k_chain)
            for ahead in range(2):
                for t in range(NT):
                    for j in range(J):
                        maxima(0, ahead, t, j, 16 * ahead + 4 * t + j)
                if ahead == 0:
                    split_shift(0, 0)

            def batch_round(i):
                rest, post, v_ahead, proj = whole(i)
                for slot in range(G * NT):
                    g, t = slot // NT, slot % NT
                    ahead = g + 2
                    if slot == 1 and rest:
                        residual_2(i - 2, 0, ps_m)
                    if slot == 2 and rest:
                        residual_2(i - 2, 1, ps_m)
                        dve.wait_ge(y2_made, 2 * (i - 1))
                        moments(y2, range(NT), y2_stats)
                        dve.wait_ge(y2_stats, i - 1)
                    if slot == 4 and rest:
                        finish_rows(i - 2)
                    if slot == 6 and post:
                        residual_1(i - 1)
                    if slot == 7 and post:
                        dve.wait_ge(y1_stats, i)
                    if slot == 8 and post:
                        dve.wait_ge(rstd1_ready, i)
                        normalize(x1, y1, range(NT), x1_made)
                    if exists(i, ahead):
                        maxima(i, ahead, t, 0, 4 * slot)
                    if slot == 2 and rest:
                        aggregate(range(NT), y2_mv)
                    if slot == 7 and post:
                        aggregate(range(NT), y1_mv)
                    if exists(i, ahead):
                        maxima(i, ahead, t, 1, 4 * slot + 1)
                    if t == 0 and exists(i, g + 1):
                        split_shift(i, g + 1)
                    if slot == 2 and post:
                        reciprocals(i - 1)
                    if slot in (10, 13, 15) and post:
                        gate_product(i - 1, (10, 13, 15).index(slot), tanh[:, :], ps_m[:, :], gated[:, :])
                    if exists(i, ahead):
                        maxima(i, ahead, t, 2, 4 * slot + 2)
                    if slot == 6 and post:
                        dve.wait_ge(y1_made, i)
                        moments(y1, range(NT), y1_stats)
                    if exists(i, ahead):
                        maxima(i, ahead, t, 3, 4 * slot + 3)

            rounds(dve, batch_round)
            n = LAST - 1
            for half in range(2):
                residual_2(n, half, ps_m)
            dve.wait_ge(y2_made, 2 * LAST)
            moments(y2, range(NT), y2_stats)
            dve.wait_ge(y2_stats, LAST)
            aggregate(range(NT), y2_mv)
            finish_rows(n)
            reciprocals(LAST)
            residual_1(LAST)
            dve.wait_ge(y1_made, B)
            moments(y1, range(NT), y1_stats)
            dve.wait_ge(y1_stats, B)
            aggregate(range(NT), y1_mv)
            dve.wait_ge(rstd1_ready, B)
            normalize(x1, y1, range(NT), x1_made)
            for c in range(C):
                gate_product(LAST, c, probs[:, 0, c, :], ps_b[:, c, :], probs[:, 1, c, :])
                dve.wait_ge(up_made, C * LAST + c + 1)
                dve.wait_ge(gated_done, C * LAST + c + 1)
                dve.wait_ge(down_made, 2 * LAST)
                dve.tensor_tensor(hidden[:, c, :], probs[:, 1, c, :], ps_a[:, c, :], ALU.mult
                                  ).then_inc(hidden_done, 1)
            dve.wait_ge(result_stored, 16 * LAST)
            for half, bank in enumerate((ps_o, ps_m)):
                ts = (2 * half, 2 * half + 1)
                residual_2(LAST, half, bank)
                dve.wait_ge(y2_made, 2 * LAST + half + 1)
                moments(y2, ts, y2_stats)
                dve.wait_ge(y2_stats, LAST + half + 1)
                aggregate(ts, y2_mv)
                dve.wait_ge(rstd2_ready, LAST + half + 1)
                normalize(result, y2, ts, result_made)

        @block.gpsimd
        def _(pool):
            pool.memset(ident[:, :], 0.0).then_inc(ident_zero, 1)
            pool.wait_ge(ident_zero, 1)
            pool.affine_select(out=ident[:, :], in_=ident[:, :], compare_op=ALU.not_equal, fill=1.0, base=0,
                               pattern=[[-1, P]], channel_multiplier=1).then_inc(ident_made, 1)
            pool.memset(k_stack[0:96, :, :, :].rearrange("p g j s -> p (g j s)").bitcast(F32), 0.0
                        ).then_inc(stacks_zero, 1)
            pool.memset(v_ones[:, :, :, :, :], 1.0).then_inc(const_made, 1)
            pool.memset(minus_half[:, :], -0.5).then_inc(const_made, 1)
            pool.memset(eps[:, :], EPS).then_inc(const_made, 1)
            pool.memset(one[:, :], 1.0).then_inc(const_made, 1)
            pool.wait_ge(const_made, 4)
            pool.wait_ge(bias_loaded, 48)

            def split_parts(n, full, rest, parts, kept, chain):
                pool.wait_ge(kept, 2 * n + 2)
                pool.tensor_tensor(rest[:, :], full[:, :], parts[:, 0, :], ALU.subtract).then_inc(chain, 1)
                pool.wait_ge(chain, 3 * n + 1)
                pool.tensor_tensor(parts[:, 1, :], rest[:, :], one[:, :].to_broadcast([P, S]), ALU.mult
                                   ).then_inc(chain, 1)
                pool.wait_ge(chain, 3 * n + 2)
                pool.tensor_tensor(parts[:, 2, :], rest[:, :], parts[:, 1, :], ALU.subtract).then_inc(chain, 1)

            def lay_values(i, ahead):
                g = ahead % G
                cols = slice(J * HD * g, J * HD * (g + 1))
                pool.wait_ge(v_kept, i + ahead // G + 1)
                pool.tensor_tensor(v_ones[:, g, :, :, 0:HD],
                                   v_rows[:, :, cols].rearrange("p t (j d) -> p t j d", j=J),
                                   v_bias[:, cols].rearrange("p (o j d) -> p o j d", o=1, j=J)
                                   .to_broadcast([P, NT, J, HD]), ALU.add).then_inc(v_filled, 1)

            def add_out_bias(n):
                pool.wait_ge(x_reloaded, 16 * n + 16)
                if not isinstance(n, int) or n >= 1:
                    pool.wait_ge(y1_made, n)
                pool.tensor_tensor(x_biased[:, :, :], x_again[:, :, :],
                                   o_bias[:, :].rearrange("p (o n) -> p o n", o=1).to_broadcast([P, NT, P]),
                                   ALU.add).then_inc(x_bias_added, 1)

            def divide_o(n):
                pool.wait_ge(recip_loaded, 16 * n + 16)
                pool.wait_ge(o_loaded, 32 * n + 32)
                if not isinstance(n, int) or n >= 1:
                    pool.wait_ge(out_made, n)
                pool.tensor_tensor(oT_norm[:, :], oT[:, :], recip_rows[:, :], ALU.mult).then_inc(o_normed, 1)

            def inverse_deviation(n, aggregated, var_ready, ready):
                pool.wait_ge(aggregated, n + 1)
                pool.tensor_tensor(var_eps[:, :], mean_var[:, :, 1], eps[:, :], ALU.add).then_inc(var_ready, 1)
                pool.wait_ge(var_ready, n + 1)
                pool.tensor_tensor(rstd[:, :], var_eps[:, :], minus_half[:, :], ALU.pow).then_inc(ready, 1)

            def multiply_up(n, c):
                pool.wait_ge(gated_done, C * n + c + 1)
                pool.wait_ge(up_kept, C * n + c + 1)
                if c == 0 and (not isinstance(n, int) or n >= 1):
                    pool.wait_ge(down_made, 2 * n)
                pool.tensor_tensor(hidden[:, c, :], gated[:, :], up_rows[:, :], ALU.mult).then_inc(hidden_done, 1)

            for ahead in range(3):
                lay_values(0, ahead)

            def batch_round(i):
                rest, post, v_ahead, proj = whole(i)
                for g in range(G):
                    if g == 0 and rest:
                        multiply_up(i - 2, 2)
                    if exists(i, g + 3):
                        if not (isinstance(i, int) and i == 0 and g == 0):
                            pool.wait_ge(pv_done, NT * (G * i + g))
                        lay_values(i, g + 3)
                    if g == 0 and rest:
                        inverse_deviation(i - 2, y2_mv, var2_ready, rstd2_ready)
                    if g == 0 and post:
                        add_out_bias(i - 1)
                    if g == 1:
                        if post:
                            divide_o(i - 1)
                        if proj:
                            split_parts(i + 2, q_full, q_rest, q_parts, q_kept, q_chain)
                        if post:
                            inverse_deviation(i - 1, y1_mv, var1_ready, rstd1_ready)
                    if g == 2 and proj:
                        split_parts(i + 2, k_full, k_rest, k_parts, k_kept, k_chain)
                    if g == 2 and post:
                        multiply_up(i - 1, 0)
                    if g == 3 and post:
                        multiply_up(i - 1, 1)

            rounds(pool, batch_round)
            multiply_up(LAST - 1, 2)
            inverse_deviation(LAST - 1, y2_mv, var2_ready, rstd2_ready)
            add_out_bias(LAST)
            divide_o(LAST)
            inverse_deviation(LAST, y1_mv, var1_ready, rstd1_ready)
            for half in range(2):
                inverse_deviation(LAST + half, y2_mv, var2_ready, rstd2_ready)


_INS = ['L0_attn_q', 'L0_attn_in_w', 'L0_attn_qkv_bias', 'L0_attn_out_w', 'L0_attn_out_b',
        'L0_ffn_w_gate', 'L0_ffn_w_up', 'L0_ffn_w_down']


def kernel(**inputs):
    import numpy as _np
    import concourse.bacc as _bacc
    from concourse import mybir as _mybir
    from concourse.bass_utils import run_bass_kernel_spmd as _run

    nc = _bacc.Bacc("TRN2", target_bir_lowering=False, num_devices=1)
    arrays, args = {}, []
    for name in _INS:
        a = _np.ascontiguousarray(inputs[name])
        arrays[f"in_{name}_dram"] = a
        args.append(nc.dram_tensor(f"in_{name}_dram", a.shape, _mybir.dt.from_np(a.dtype), kind="ExternalInput").ap())
    shape = inputs['L0_attn_q'].shape
    out = nc.dram_tensor("out_0_dram", shape, _mybir.dt.from_np(_np.dtype('float32')), kind="ExternalOutput").ap()
    transformer_layer(nc, *args, out)
    r = _run(nc, [arrays], core_ids=[0])
    return r.results[0]["out_0_dram"]
```

```python
from contextlib import ExitStack

import numpy as np

import concourse.bass as bass
from concourse import mybir

ALU = mybir.AluOpType
ACT = mybir.ActivationFunctionType
AX = mybir.AxisListType
F32 = mybir.dt.float32
BF16 = mybir.dt.bfloat16
I32 = mybir.dt.int32

P = 128
H = 16
HD = 8
G = 4
J = H // G
NT = 4
EPS = 1e-5
WEIGHT_SCALE = 1.0 / 127.0
PRODUCTS = 6
ROWS = HD * PRODUCTS
SHIFT_ROW = 96
SCORE_ROWS = 96
BANKS = 3
OROWS = 32


TWO_ONES = float(np.uint32(0x3F803F80).view(np.float32))


def transformer_layer(nc, x, in_w, qkv_bias, out_w, out_b, w_gate, w_up, w_down, out):
    B, S, D = x.shape
    HID = w_gate.shape[0]
    C = HID // P
    assert D == P and S == NT * P and HID == C * P and D == H * HD
    SCALING = float(HD) ** 0.5

    q_scratch = nc.dram_tensor("q_scratch", (B, P, PRODUCTS, S), BF16, kind="Internal").ap()
    k_scratch = nc.dram_tensor("k_scratch", (B, P, PRODUCTS, S), BF16, kind="Internal").ap()
    o_scratch = nc.dram_tensor("o_scratch", (B, H, OROWS, S), F32, kind="Internal").ap()
    r_scratch = nc.dram_tensor("r_scratch", (B, H, S), F32, kind="Internal").ap()

    x_rows = x.rearrange("b (t p) d -> b p t d", p=P)
    out_rows = out.rearrange("b (t p) d -> b p t d", p=P)
    q_stacks = q_scratch.rearrange("b (g j d) c s -> b g (d c) j s", g=G, j=J)
    k_stacks = k_scratch.rearrange("b (g j d) c s -> b g (d c) j s", g=G, j=J)

    with ExitStack() as ctx:
        def sb(name, shape, dt=F32):
            return ctx.enter_context(nc.sbuf_tensor(name, shape, dt))

        def psum(name, shape):
            return ctx.enter_context(nc.psum_tensor(name, shape, F32))

        def sem(name):
            return ctx.enter_context(nc.semaphore(name))

        ident = sb("ident", [P, P])
        in_w_sb = sb("in_w_sb", [P, 3, P])
        out_w_sb = sb("out_w_sb", [P, P])
        w_int = sb("w_int", [P, 3, C, P], I32)
        w_deq = sb("w_deq", [P, 3, C, P])
        wT = sb("wT", [P, 4, P])
        gateT = sb("gateT", [P, C * P])
        upT = sb("upT", [P, C * P])
        downT = sb("downT", [P, C, P])
        bias_col = sb("bias_col", [P, 3])
        bias_q = sb("bias_q", [P, 1])
        v_bias = sb("v_bias", [P, P])
        o_bias = sb("o_bias", [P, P])
        minus_half = sb("minus_half", [P, NT])
        eps = sb("eps", [P, NT])
        one = sb("one", [P, 1])
        x_in = sb("x_in", [P, NT, P])
        xT = sb("xT", [P, S])
        q_full = sb("q_full", [P, S])
        k_full = sb("k_full", [P, S])
        q_rest = sb("q_rest", [P, S])
        k_rest = sb("k_rest", [P, S])
        q_parts = sb("q_parts", [P, 3, S], BF16)
        k_parts = sb("k_parts", [P, 3, S], BF16)
        v_rows = sb("v_rows", [P, NT, P])
        q_stack = sb("q_stack", [P, G, J, S], BF16)
        k_stack = sb("k_stack", [P, G, J, S], BF16)
        v_ones = sb("v_ones", [P, G, NT, J, OROWS])
        neg_max = sb("neg_max", [P, 2, J * NT])
        shift_parts = sb("shift_parts", [J * NT, 2, P], BF16)
        probs = sb("probs", [P, 2, J, S])
        o_raw = sb("o_raw", [P, 2, S])
        oT = sb("oT", [P, S])
        sums = sb("sums", [P, H * S // P])
        recips = sb("recips", [P, H * S // P])
        recip_rows = sb("recip_rows", [P, S])
        oT_norm = sb("oT_norm", [P, S])
        x_again = sb("x_again", [P, NT, P])
        x_biased = sb("x_biased", [P, NT, P])
        y1 = sb("y1", [P, NT, P])
        y2 = sb("y2", [P, NT, P])
        norm1, norm2 = ([sb(f"{name}{k}", [P, NT, *width]) for name, width in
                         (("stats", (6,)), ("mean_var", (2,)), ("var_eps", ()), ("rstd", ()))] for k in (1, 2))
        x1 = sb("x1", [P, NT, P])
        x1T = sb("x1T", [P, S])
        tanh = sb("tanh", [P, S])
        gated = sb("gated", [P, S])
        up_rows = sb("up_rows", [P, S])
        hidden = sb("hidden", [P, C, S])
        result = sb("result", [P, NT, P])
        recip_cols = sb("recip_cols", [P, G, NT, J])
        o_rows = sb("o_rows", [P, NT, P])

        ps_b = psum("ps_b", [P, BANKS, S])
        ps_a = psum("ps_a", [P, BANKS, S])
        ps_o = psum("ps_o", [P, S])
        ps_m = psum("ps_m", [P, S])

        w_loaded = sem("w_loaded")
        out_w_loaded = sem("out_w_loaded")
        bias_loaded = sem("bias_loaded")
        x_loaded = sem("x_loaded")
        ident_zero = sem("ident_zero")
        ident_made = sem("ident_made")
        stack0_set = sem("stack0_set")
        stacks_set = sem("stacks_set")
        const_made = sem("const_made")
        bias_q_made = sem("bias_q_made")
        w_scaled = sem("w_scaled")
        w_transposed = sem("w_transposed")
        w_ready = sem("w_ready")
        ffn_w_loaded = sem("ffn_w_loaded")
        xT_made = sem("xT_made")
        xT_kept = sem("xT_kept")
        q_made = sem("q_made")
        k_made = sem("k_made")
        q_kept = sem("q_kept")
        k_kept = sem("k_kept")
        q_chain = sem("q_chain")
        k_chain = sem("k_chain")
        v_made = sem("v_made")
        v_kept = sem("v_kept")
        v_filled = sem("v_filled")
        q_stored = sem("q_stored")
        k_stored = sem("k_stored")
        stack_filled = [sem(f"stack_filled{g}") for g in range(G)]
        shift_filled = [sem(f"shift_filled{g}") for g in range(G)]
        a_scored = sem("a_scored")
        a_reduced = sem("a_reduced")
        shift_turned = sem("shift_turned")
        shift_split = sem("shift_split")
        b_scored = sem("b_scored")
        exp_done = sem("exp_done")
        pv_done = sem("pv_done")
        o_kept = sem("o_kept")
        o_stored = [sem(f"o_stored{n}") for n in range(2)]
        o_loaded = sem("o_loaded")
        recip_done = sem("recip_done")
        recip_stored = sem("recip_stored")
        recip_loaded = sem("recip_loaded")
        o_normed = sem("o_normed")
        o_turned = sem("o_turned")
        recip_cols_made = sem("recip_cols_made")
        o_rows_made = sem("o_rows_made")
        o_rows_turned = sem("o_rows_turned")
        o_rows_kept = sem("o_rows_kept")
        x_reloaded = sem("x_reloaded")
        x_bias_added = sem("x_bias_added")
        out_made = sem("out_made")
        y1_made = sem("y1_made")
        y1_stats = sem("y1_stats")
        y1_mv = sem("y1_mv")
        var1_ready = sem("var1_ready")
        rstd1_ready = sem("rstd1_ready")
        x1_made = sem("x1_made")
        x1T_made = sem("x1T_made")
        x1T_kept = sem("x1T_kept")
        gate_made = sem("gate_made")
        tanh_done = sem("tanh_done")
        gated_done = sem("gated_done")
        up_made = sem("up_made")
        up_kept = sem("up_kept")
        hidden_done = sem("hidden_done")
        down_made = sem("down_made")
        y2_made = sem("y2_made")
        y2_stats = sem("y2_stats")
        y2_mv = sem("y2_mv")
        var2_ready = sem("var2_ready")
        rstd2_ready = sem("rstd2_ready")
        result_made = sem("result_made")
        result_free = sem("result_free")

        LAST = B - 1
        EARLY = 2 * 16 - G * NT // 2

        CATCH_UP_TURNS = (2, 6, 9, 13)
        UP_BANKS = (2, 0, 1)

        def is_first(i):
            return isinstance(i, int) and i == 0

        def is_last(i):
            return isinstance(i, int) and i == LAST

        def whole(i):
            known = isinstance(i, int)
            rest = not known or i >= 2
            post = not known or i >= 1
            v_ahead = not known or 1 <= i <= LAST - 1
            proj = not known or 1 <= i <= LAST - 2
            return rest, post, v_ahead, proj

        def since(tile, before):
            if tile >= BANKS or before == 0:
                return BANKS
            return min(n for n in range(tile + 1, tile + before + 1) if (before + tile - n) % BANKS == tile % BANKS)

        def exists(i, unit_ahead):
            return not isinstance(i, int) or G * i + unit_ahead < G * B

        def tiles_of(i, slot, j):
            if is_first(i):
                extra = (slot + 1) // 2
                first = EARLY + 4 * slot + j + extra
                count = 2 if j == J - 1 and slot % 2 == 0 else 1
                return [(a // 16, a // 4 % 4, a % 4, a) for a in range(first, first + count)]
            ahead = slot // NT + 2
            return [(ahead, slot % NT, j, 4 * slot + j)] if exists(i, ahead) else []

        def rows(half):
            return (2 * half, 2 * half + 1), slice(2 * half * P, 2 * (half + 1) * P)

        def rounds(eng, batch_round):
            batch_round(0)
            batch_round(1)
            with eng.Fori(2, B - 2) as i:
                batch_round(i)
            batch_round(B - 2)
            batch_round(B - 1)

        block = ctx.enter_context(nc.Block())

        @block.sync
        def _(sp):
            sp.dma_start(x_in[:, :, :], x_rows[0]).then_inc(x_loaded, 16)
            sp.dma_start(in_w_sb[:, :, :], in_w.rearrange("(c p) d -> p c d", p=P)).then_inc(w_loaded, 16)
            sp.dma_start(out_w_sb[:, :], out_w).then_inc(out_w_loaded, 16)
            sp.dma_start(w_int[:, 0, :, :], w_gate.rearrange("(c p) d -> p c d", p=P)).then_inc(ffn_w_loaded, 16)
            sp.dma_start(w_int[:, 1, :, :], w_up.rearrange("(c p) d -> p c d", p=P)).then_inc(ffn_w_loaded, 16)
            sp.dma_start(w_int[:, 2, :, :], w_down.rearrange("p (c n) -> p c n", c=C)).then_inc(ffn_w_loaded, 16)

            def load_x(n):
                sp.wait_ge(xT_made, n)
                sp.dma_start(x_in[:, :, :], x_rows[n]).then_inc(x_loaded, 16)

            def store_q(n):
                groups = ((5, 6), (3, 5), (0, 3)) if isinstance(n, int) else ((0, 3), (3, 5), (5, 6))
                for c, end in groups:
                    if not isinstance(n, int):
                        if c == 0:
                            sp.wait_ge(q_chain, 3 * n + 3)
                    elif c == 5:
                        sp.wait_ge(q_kept, 2 * n + 2)
                    else:
                        sp.wait_ge(q_chain, 3 * n + end - c)
                    sp.dma_start(q_scratch[n, :, c:end, :], q_parts[:, 0:end - c, :]).then_inc(q_stored, 16)

            def store_k(n):
                for part, c, end in ((0, 0, 3), (1, 3, 5), (2, 5, 6)):
                    if not isinstance(n, int):
                        if part == 0:
                            sp.wait_ge(k_chain, 3 * n + 3)
                    elif part == 0:
                        sp.wait_ge(k_kept, 2 * n + 2)
                    else:
                        sp.wait_ge(k_chain, 3 * n + 1 + part)
                    sp.dma_start(k_scratch[n, :, c:end, :],
                                 k_parts[:, part:part + 1, :].to_broadcast([P, end - c, S])).then_inc(k_stored, 16)

            def fill_stacks(i, ahead):
                n, g = i + ahead // G, ahead % G
                if g == 0 or isinstance(i, int):
                    sp.wait_ge(q_stored, 48 * n + 48)
                sp.dma_start(q_stack[0:ROWS, g, :, :], q_stacks[n, g]).then_inc(stack_filled[g], 16)
                if g == 0 or isinstance(i, int):
                    sp.wait_ge(k_stored, 48 * n + 48)
                sp.dma_start(k_stack[0:ROWS, g, :, :], k_stacks[n, g]).then_inc(stack_filled[g], 16)

            def fill_shift(i, ahead):
                g = ahead % G
                sp.wait_ge(shift_split, 2 * (G * i + ahead) + 2)
                for c in range(2):
                    row = q_stack[SHIFT_ROW + c:SHIFT_ROW + c + 1, g, :, :].rearrange("o j s -> o (j s)")
                    sp.dma_start(row, shift_parts[:, c, :]).then_inc(shift_filled[g], 16)

            def store_o(i, behind):
                g = G - behind
                sp.wait_ge(o_kept, G * i + g + 1)
                sp.dma_start(o_scratch[i, J * g:J * g + J].rearrange("j r s -> (j r) s"), o_raw[:, g % 2, :]
                             ).then_inc(o_stored[g % 2], 16)

            def normalizer(n):
                sp.wait_ge(o_stored[0], 32 * n + 32)
                sp.wait_ge(o_stored[1], 32 * n + 32)
                sp.dma_start(sums[:, :], o_scratch[n, :, HD, :].rearrange("h (c w) -> h c w", c=P // H)
                             ).then_inc(o_loaded, 16)
                sp.dma_start(oT[:, :], o_scratch[n, :, 0:HD, :]).then_inc(o_loaded, 16)
                sp.wait_ge(recip_done, n + 1)
                sp.dma_start(r_scratch[n].rearrange("h (c w) -> (h c) w", c=P // H), recips[:, :]
                             ).then_inc(recip_stored, 16)
                sp.wait_ge(recip_stored, 16 * n + 16)
                sp.dma_start(recip_rows[:, :],
                             r_scratch[n].rearrange("h (o s) -> h o s", o=1).to_broadcast([H, HD, S])
                             ).then_inc(recip_loaded, 16)

            def reload_x(n):
                if not isinstance(n, int) or n >= 1:
                    sp.wait_ge(x_bias_added, n)
                sp.dma_start(x_again[:, :, :], x_rows[n]).then_inc(x_reloaded, 16)

            def store_result(n):
                sp.wait_ge(result_made, n + 1)
                sp.dma_start(out_rows[n], result[:, :, :]).then_inc(result_free, 16)

            load_x(1)
            store_q(0)
            store_k(0)
            sp.wait_ge(stack0_set, 2)
            fill_stacks(0, 0)
            load_x(2)
            sp.wait_ge(stacks_set, 2)
            fill_stacks(0, 1)
            fill_stacks(0, 2)
            store_q(1)
            store_k(1)
            fill_shift(0, 0)
            store_q(2)
            store_k(2)

            def batch_round(i):
                rest, post, v_ahead, proj = whole(i)
                for g in range(G):
                    if exists(i, g + 3):
                        if not (is_first(i) and g == 0):
                            sp.wait_ge(b_scored, 16 * (G * i + g))
                        fill_stacks(i, g + 3)
                    if g == 0 and proj:
                        load_x(i + 2)
                    if g > 0:
                        if not is_last(i):
                            store_o(i, G - g + 1)
                    elif post:
                        store_o(i - 1, 1)
                    if exists(i, g + 1) and not is_first(i):
                        fill_shift(i, g + 1)
                    if g == 0 and post:
                        reload_x(i - 1)
                        normalizer(i - 1)
                    if g == 2 and is_last(i):
                        reload_x(i)
                    if g == 2 and proj:
                        store_q(i + 2)
                    if g == 3 and proj:
                        store_k(i + 2)
                    if g == 3 and rest:
                        store_result(i - 2)
                    if is_first(i):
                        fill_shift(i, g + 1)

            rounds(sp, batch_round)
            store_result(LAST - 1)
            for half in range(2):
                ts = slice(2 * half, 2 * half + 2)
                sp.wait_ge(result_made, LAST + half + 1)
                sp.dma_start(out_rows[LAST, :, ts, :], result[:, ts, :]).then_inc(result_free, 16)
            sp.wait_ge(result_free, 16 * (B + 2))

        @block.tensor
        def _(pe):
            pe.wait_ge(ident_made, 1)

            def keep_warm(count, bank):
                for _ in range(count):
                    pe.matmul(bank[:, 0:P], ident[:, :], ident[:, :], start=True, stop=True)

            def turn_ffn_weights():
                for w in range(3):
                    pe.wait_ge(w_scaled, w + 1)
                    if w == 0:
                        pe.wait_ge(w_ready, 2)
                    for c in range(C):
                        last = pe.transpose(ps_b[:, w, c * P:(c + 1) * P], w_deq[:, w, c, :], ident[:, :])
                    last.then_inc(w_transposed, 1)

            def turn_x(n, bank=ps_m):
                pe.wait_ge(x_loaded, 16 * n + 16)
                for t in range(NT):
                    last = pe.transpose(bank[:, t * P:(t + 1) * P], x_in[:, t, :], ident[:, :])
                last.then_inc(xT_made, 1)

            def project_q(n, bank):
                pe.wait_ge(xT_kept, n + 1)
                pe.matmul(bank, wT[:, 0, :], xT[:, :], start=True, stop=True).then_inc(q_made, 1)

            def project_k(n, bank):
                pe.matmul(bank, wT[:, 1, :], xT[:, :], start=True, stop=True).then_inc(k_made, 1)

            def project_v(bank):
                for t in range(NT):
                    last = pe.matmul(bank[:, t * P:(t + 1) * P], xT[:, t * P:(t + 1) * P], wT[:, 2, :],
                                     start=True, stop=True)
                last.then_inc(v_made, 1)

            def score_a(i, ahead, t, j, tile, before):
                g = ahead % G
                a = 16 * (G * i + ahead) + 4 * t + j
                free = a - since(tile, before) + 1
                if not isinstance(free, int) or free > 0:
                    pe.wait_ge(a_reduced, free)
                pe.matmul(ps_a[:, tile % BANKS, :], q_stack[0:SCORE_ROWS, g, j, t * P:(t + 1) * P],
                          k_stack[0:SCORE_ROWS, g, j, :], start=True, stop=True).then_inc(a_scored, 1)

            def wait_stack(i, ahead):
                pe.wait_ge(stack_filled[ahead % G], 32 * (i + ahead // G) + 32)

            def score_b(i, g, t, j):
                tile = 4 * (NT * g + t) + j
                free = 64 * i + tile - since(tile, 64) + 1
                if not isinstance(free, int) or free > 0:
                    pe.wait_ge(exp_done, free)
                pe.matmul(ps_b[:, tile % BANKS, :], k_stack[:, g, j, t * P:(t + 1) * P], q_stack[:, g, j, :],
                          start=True, stop=True).then_inc(b_scored, 1)

            def weigh_values(i, slot):
                g, t = slot // NT, slot % NT
                pe.wait_ge(exp_done, 4 * (16 * i + slot) + 4)
                if t == 0:
                    pe.wait_ge(v_filled, G * i + g + 1)
                    if not is_first(i):
                        if exists(i, g + 1):
                            split_of(i, g + 1)
                        else:
                            pe.wait_ge(o_kept, G * i + g)
                    elif g >= 1:
                        pe.wait_ge(o_kept, g)
                    else:
                        pe.wait_ge(q_kept, 6)
                for j in range(J):
                    last = pe.matmul(ps_o[OROWS * j:OROWS * j + OROWS, :], v_ones[:, g, t, j, :],
                                     probs[:, t % 2, j, :], start=(t == 0), stop=(t == NT - 1))
                last.then_inc(pv_done, 1)

            def turn_shift(i, ahead, bank):
                pe.wait_ge(a_reduced, 16 * (G * i + ahead) + 16)
                pe.transpose(bank[0:J * NT, 0:P], neg_max[:, ahead % 2, :], ident[:, :]).then_inc(shift_turned, 1)

            def project_out(ts, bank):
                for t in ts:
                    last = pe.matmul(bank[:, t * P:(t + 1) * P], oT_norm[:, t * P:(t + 1) * P], wT[:, 3, :],
                                     start=True, stop=True)
                last.then_inc(out_made, 1)

            def turn_x1(ts, bank):
                for t in ts:
                    last = pe.transpose(bank[:, t * P:(t + 1) * P], x1[:, t, :], ident[:, :])
                last.then_inc(x1T_made, 1)

            def gate(c, cols, bank):
                pe.matmul(bank[:, cols], gateT[:, c * P:(c + 1) * P], x1T[:, cols], start=True, stop=True
                          ).then_inc(gate_made, 1)

            def up(c, cols, bank):
                pe.matmul(bank[:, cols], upT[:, c * P:(c + 1) * P], x1T[:, cols], start=True, stop=True
                          ).then_inc(up_made, 1)

            def turn_outputs(g):
                pe.wait_ge(o_kept, G * LAST + g + 1)
                pe.wait_ge(a_reduced, 16 * G * B)
                if g >= 2:
                    pe.wait_ge(hidden_done, C * (LAST - 1) + UP_BANKS.index(g % BANKS) + 1)
                for t in range(NT):
                    last = pe.transpose(ps_a[:, g % BANKS, t * P:(t + 1) * P], o_raw[:, g % 2, t * P:(t + 1) * P],
                                        ident[:, :])
                last.then_inc(o_turned, 1)

            def down(half, bank):
                down_tiles(rows(half)[0], bank).then_inc(down_made, 1)

            def down_tiles(ts, bank):
                for t in ts:
                    for c in range(C):
                        last = pe.matmul(bank[:, t * P:(t + 1) * P], hidden[:, c, t * P:(t + 1) * P],
                                         downT[:, c, :], start=(c == 0), stop=(c == C - 1))
                return last

            turn_x(0)
            pe.wait_ge(w_loaded, 16)
            for c in range(2):
                last = pe.transpose(ps_b[:, 0, c * P:(c + 1) * P], in_w_sb[:, c, :], ident[:, :])
            last.then_inc(w_transposed, 1)
            pe.wait_ge(out_w_loaded, 16)
            pe.transpose(ps_b[:, 1, 0:P], in_w_sb[:, 2, :], ident[:, :])
            pe.transpose(ps_b[:, 1, P:2 * P], out_w_sb[:, :], ident[:, :]).then_inc(w_transposed, 1)
            pe.wait_ge(w_ready, 1)
            project_q(0, ps_a[:, 0, :])
            project_k(0, ps_a[:, 1, :])
            turn_x(1)
            pe.wait_ge(w_ready, 2)
            project_v(ps_a[:, 2, :])
            turn_ffn_weights()
            project_q(1, ps_o[:, :])
            project_k(1, ps_m[:, :])
            pe.wait_ge(w_ready, 5)
            project_v(ps_b[:, 0, :])
            pe.wait_ge(v_kept, 1)
            for a in range(EARLY):
                if a == 4:
                    turn_x(2, ps_b[:, 1, :])
                if a == 8:
                    pe.wait_ge(q_kept, 4)
                    project_q(2, ps_o[:, :])
                if a == 12:
                    pe.wait_ge(k_kept, 4)
                    project_k(2, ps_m[:, :])
                if a % 16 == 0:
                    wait_stack(0, a // 16)
                score_a(0, a // 16, a // 4 % 4, a % 4, a, 0)
                if a == 16:
                    turn_shift(0, 0, ps_b[:, 2, :])
            pe.wait_ge(v_kept, 2)
            pe.wait_ge(xT_kept, 3)

            def split_of(i, ahead):
                pe.wait_ge(shift_split, 2 * (G * i + ahead) + 2)

            def misc(i, slot):
                rest, post, v_ahead, proj = whole(i)
                n = i - 1
                if slot == 0 and v_ahead:
                    if rest:
                        up_taken(i - 2, C - 1)
                    else:
                        split_of(i, 0)
                    project_v(ps_m)
                if slot == 1 and rest:
                    if v_ahead:
                        pe.wait_ge(v_kept, i + 2)
                    else:
                        up_taken(i - 2, C - 1)
                    pe.wait_ge(hidden_done, C * (i - 2) + C)
                    down(0, ps_m)
                if slot == 2 and rest:
                    pe.wait_ge(y2_made, 2 * (i - 2) + 1)
                    down(1, ps_m)
                if slot == 3 and proj:
                    if rest:
                        pe.wait_ge(y2_made, 2 * (i - 1))
                    else:
                        pe.wait_ge(v_kept, i + 2)
                    turn_x(i + 2)
                if slot == 4 and proj:
                    project_q(i + 2, ps_m[:, :])
                if slot == 5 and post:
                    if proj:
                        pe.wait_ge(q_kept, 2 * (i + 2) + 2)
                    else:
                        pe.wait_ge(y2_made, 2 * (i - 1))
                    pe.wait_ge(o_normed, i)
                    project_out(range(NT), ps_m)
                if slot == 6 and proj:
                    pe.wait_ge(y1_made, i)
                    project_k(i + 2, ps_m[:, :])
                whole_bank = slice(0, S)
                if slot == 8 and post:
                    if proj:
                        pe.wait_ge(k_kept, 2 * (i + 2) + 2)
                    pe.wait_ge(x1_made, i)
                    turn_x1(range(NT), ps_m)
                if is_last(i):
                    c = (slot - 9) // 2
                    if slot in (9, 11, 13):
                        if c == 0:
                            pe.wait_ge(x1T_kept, i)
                        else:
                            pe.wait_ge(gated_done, C * n + c)
                        gate(c, whole_bank, ps_m)
                    if slot in (10, 12, 14):
                        if c == 0:
                            pe.wait_ge(a_reduced, 16 * G * B)
                        else:
                            pe.wait_ge(o_rows_made, c)
                        up(c, whole_bank, ps_a[:, UP_BANKS[c], :])
                    if slot in (8, 9, 13):
                        turn_outputs((8, 9, 13).index(slot))
                    if slot == 15:
                        pe.wait_ge(hidden_done, C * LAST)
                        down(0, ps_m)
                    return
                if slot == 9 and post:
                    pe.wait_ge(x1T_kept, i)
                    gate(0, whole_bank, ps_m)
                if slot == 10 and post:
                    pe.wait_ge(gated_done, C * n + 1)
                    up(0, whole_bank, ps_m)
                if slot == 12 and post:
                    up_taken(n, 0)
                    gate(1, whole_bank, ps_m)
                if slot == 13 and post:
                    pe.wait_ge(gated_done, C * n + 2)
                    up(1, whole_bank, ps_m)
                if slot == 14 and post:
                    up_taken(n, 1)
                    gate(2, whole_bank, ps_m)
                if slot == 15 and post:
                    pe.wait_ge(gated_done, C * n + 3)
                    up(2, whole_bank, ps_m)

            def up_taken(n, c):
                pe.wait_ge(up_kept, C * n + c + 1)

            def batch_round(i):
                before = {0: 0, 1: 6 * 16}.get(i, 64) if isinstance(i, int) else 64
                for slot in range(G * NT):
                    g, t = slot // NT, slot % NT
                    if t == 0:
                        pe.wait_ge(shift_filled[g], 32 * i + 32)
                    for j in range(J):
                        for ahead, query, head, tile in tiles_of(i, slot, j):
                            if query == 0 and head == 0:
                                wait_stack(i, ahead)
                            score_a(i, ahead, query, head, tile, before)
                        score_b(i, g, t, j)
                        if j == 1:
                            if slot > 0:
                                weigh_values(i, slot - 1)
                            elif not isinstance(i, int) or i > 0:
                                weigh_values(i - 1, G * NT - 1)
                            if is_first(i) and slot in CATCH_UP_TURNS:
                                ahead = CATCH_UP_TURNS.index(slot) + 1
                                split_of(i, ahead - 1)
                                if ahead == 1:
                                    pe.wait_ge(k_kept, 6)
                                turn_shift(i, ahead, ps_m)
                    if t == 0 and not is_first(i) and exists(i, g + 1):
                        pe.wait_ge(o_kept, G * i + g)
                        turn_shift(i, g + 1, ps_o)
                    misc(i, slot)

            rounds(pe, batch_round)
            weigh_values(LAST, G * NT - 1)
            down_tiles((2,), ps_b[:, 0, :])
            turn_outputs(G - 1)
            down_tiles((3,), ps_b[:, 0, :]).then_inc(down_made, 1)
            pe.wait_ge(o_rows_made, G)
            for half, bank in enumerate((ps_o, ps_a[:, 1, :])):
                for t in rows(half)[0]:
                    last = pe.transpose(bank[:, t * P:(t + 1) * P], o_rows[:, t, :], ident[:, :])
                last.then_inc(o_rows_turned, 1)
            keep_warm(3, ps_b[:, 2, :])
            for half, bank in enumerate((ps_a[:, 2, :], ps_m)):
                pe.wait_ge(o_rows_kept, half + 1)
                pe.wait_ge(y2_made, 2 * (LAST - 1) + 1)
                project_out(rows(half)[0], bank)
            keep_warm(14, ps_b[:, 2, :])
            for half, bank in enumerate((ps_o, ps_m)):
                pe.wait_ge(x1_made, LAST + half + 1)
                turn_x1(rows(half)[0], bank)
                if half == 0:
                    keep_warm(2, ps_b[:, 2, :])
            pe.wait_ge(y2_made, 2 * LAST)
            for half in range(2):
                cols = rows(half)[1]
                pe.wait_ge(x1T_kept, LAST + half + 1)
                for c in range(C):
                    if half:
                        pe.wait_ge(gated_done, C * LAST + c + 1)
                    gate(c, cols, ps_b[:, c, :])
                    if half:
                        pe.wait_ge(hidden_done, C * LAST + c + 1)
                    up(c, cols, ps_a[:, c, :])
            for half, bank in enumerate((ps_o, ps_m)):
                pe.wait_ge(hidden_done, C * (LAST + half) + C)
                down(half, bank)

        @block.scalar
        def _(act):
            with nc.allow_non_contiguous_dma(reason="a bias per partition, 384 numbers once"):
                act.dma_start(bias_col[:, :], qkv_bias.rearrange("(c p) -> p c", p=P)).then_inc(bias_loaded, 16)
            bias_2d = qkv_bias.rearrange("(a n) -> a n", a=1)
            act.dma_start(v_bias[:, :], bias_2d[:, 2 * P:3 * P].to_broadcast([P, P])).then_inc(bias_loaded, 16)
            act.dma_start(o_bias[:, :], out_b.rearrange("(a n) -> a n", a=1).to_broadcast([P, P])
                          ).then_inc(bias_loaded, 16)

            def keep_weights(w, dst, src):
                act.wait_ge(w_transposed, w + 1)
                act.copy(dst, src).then_inc(w_ready, 1)

            def keep_xT(n, bank=ps_m[:, :]):
                act.wait_ge(xT_made, n + 1)
                if not isinstance(n, int) or n >= 1:
                    act.wait_ge(v_made, n)
                act.copy(xT[:, :], bank).then_inc(xT_kept, 1)

            def keep_q(n, bank):
                act.wait_ge(q_made, n + 1)
                if not isinstance(n, int) or n >= 1:
                    act.wait_ge(q_stored, 48 * n)
                act.activation(q_full[:, :], bank, ACT.Identity, bias=bias_q[:, :], scale=1.0 / SCALING
                               ).then_inc(q_kept, 1)
                act.activation(q_parts[:, 0, :], bank, ACT.Identity, bias=bias_q[:, :], scale=1.0 / SCALING
                               ).then_inc(q_kept, 1)

            def keep_k(n, bank):
                act.wait_ge(k_made, n + 1)
                if not isinstance(n, int) or n >= 1:
                    act.wait_ge(k_stored, 48 * n)
                act.activation(k_full[:, :], bank, ACT.Identity, bias=bias_col[:, 1:2]).then_inc(k_kept, 1)
                act.activation(k_parts[:, 0, :], bank, ACT.Identity, bias=bias_col[:, 1:2]
                               ).then_inc(k_kept, 1)

            def keep_v(n, bank):
                act.wait_ge(v_made, n + 1)
                if not isinstance(n, int) or n >= 1:
                    act.wait_ge(v_filled, G * n)
                act.copy(v_rows[:, :, :].rearrange("p t n -> p (t n)"), bank).then_inc(v_kept, 1)

            def exponentials(i, slot, j):
                s = 16 * i + slot
                act.wait_ge(b_scored, 4 * s + j + 1)
                if j == 0 and (not isinstance(s, int) or s >= 2):
                    act.wait_ge(pv_done, s - 1)
                act.activation(probs[:, slot % 2, j, :], ps_b[:, (4 * slot + j) % BANKS, :], ACT.Exp
                               ).then_inc(exp_done, 1)

            def keep_o(i, g):
                act.wait_ge(pv_done, NT * (G * i + g) + NT)
                if is_last(i) and g >= 2:
                    act.wait_ge(o_turned, g - 1)
                elif not isinstance(i, int) or G * i + g >= 2:
                    act.wait_ge(o_stored[g % 2], 16 * (2 * i + g // 2))
                act.copy(o_raw[:, g % 2, :], ps_o[:, :]).then_inc(o_kept, 1)

            def keep_x1T(n):
                act.wait_ge(x1T_made, n + 1)
                act.copy(x1T[:, :], ps_m[:, :]).then_inc(x1T_kept, 1)

            def gate_tanh(n, c):
                act.wait_ge(gate_made, C * n + c + 1)
                if not isinstance(n, int) or C * n + c >= 1:
                    act.wait_ge(gated_done, C * n + c)
                act.activation(tanh[:, :], ps_m[:, :], ACT.Tanh, scale=0.5).then_inc(tanh_done, 1)

            def keep_up(n, c):
                act.wait_ge(up_made, C * n + c + 1)
                if not isinstance(n, int) or C * n + c >= 1:
                    act.wait_ge(hidden_done, C * n + c)
                act.copy(up_rows[:, :], ps_m[:, :]).then_inc(up_kept, 1)

            keep_xT(0)
            keep_weights(0, wT[:, 0:2, :].rearrange("p c n -> p (c n)"), ps_b[:, 0, 0:2 * P])
            act.wait_ge(bias_loaded, 48)
            act.mul(bias_q[:, :], bias_col[:, 0:1], 1.0 / SCALING).then_inc(bias_q_made, 1)
            keep_weights(1, wT[:, 2:4, :].rearrange("p c n -> p (c n)"), ps_b[:, 1, 0:2 * P])
            act.wait_ge(bias_q_made, 1)
            keep_q(0, ps_a[:, 0, :])
            keep_k(0, ps_a[:, 1, :])
            keep_v(0, ps_a[:, 2, :])
            keep_xT(1)
            keep_weights(2, gateT[:, :], ps_b[:, 0, 0:C * P])
            keep_weights(3, upT[:, :], ps_b[:, 1, 0:C * P])
            keep_weights(4, downT[:, :, :].rearrange("p c n -> p (c n)"), ps_b[:, 2, 0:C * P])
            keep_q(1, ps_o[:, :])
            keep_v(1, ps_b[:, 0, :])
            keep_k(1, ps_m[:, :])
            keep_xT(2, ps_b[:, 1, :])
            keep_q(2, ps_o[:, :])
            keep_k(2, ps_m[:, :])

            def batch_round(i):
                rest, post, v_ahead, proj = whole(i)
                for slot in range(G * NT):
                    g, t = slot // NT, slot % NT
                    exponentials(i, slot, 0)
                    if rest and slot == 0:
                        keep_up(i - 2, 2)
                    if v_ahead and slot == 1:
                        keep_v(i + 1, ps_m[:, :])
                    if proj and slot == 4:
                        keep_xT(i + 2)
                    if proj and slot == 5:
                        keep_q(i + 2, ps_m[:, :])
                    if proj and slot == 7:
                        keep_k(i + 2, ps_m[:, :])
                    if post and slot == 9 and not is_last(i):
                        keep_x1T(i - 1)
                    gates = (10, 12, 14) if is_last(i) else (10, 13, 15)
                    if post and slot in gates:
                        gate_tanh(i - 1, gates.index(slot))
                    if post and slot in (11, 14) and not is_last(i):
                        keep_up(i - 1, (11, 14).index(slot))
                    exponentials(i, slot, 1)
                    if t == 0 and g > 0:
                        keep_o(i, g - 1)
                    elif t == 0 and (not isinstance(i, int) or i > 0):
                        keep_o(i - 1, G - 1)
                    exponentials(i, slot, 2)
                    exponentials(i, slot, 3)

            rounds(act, batch_round)
            keep_o(LAST, G - 1)
            for half, bank in enumerate((ps_o, ps_a[:, 1, :])):
                cols = rows(half)[1]
                act.wait_ge(o_rows_turned, half + 1)
                act.wait_ge(out_made, LAST)
                act.copy(oT_norm[:, cols], bank[:, cols]).then_inc(o_rows_kept, 1)
            for half, bank in enumerate((ps_o, ps_m)):
                cols = rows(half)[1]
                act.wait_ge(x1T_made, LAST + half + 1)
                act.copy(x1T[:, cols], bank[:, cols]).then_inc(x1T_kept, 1)
            for half in range(2):
                cols = rows(half)[1]
                for c in range(C):
                    act.wait_ge(gate_made, C * (LAST + half) + c + 1)
                    act.activation(probs[:, 0, c, cols], ps_b[:, c, cols], ACT.Tanh, scale=0.5
                                   ).then_inc(tanh_done, 1)

        @block.vector
        def _(dve):
            dve.memset(result[:, 0, 0:1], 0.0).then_inc(result_free, 16)
            dve.memset(q_stack[:, 0, :, :].rearrange("p j s -> p (j s)").bitcast(F32), 0.0).then_inc(stack0_set, 1)
            dve.memset(k_stack[:, 0, :, :].rearrange("p j s -> p (j s)").bitcast(F32), TWO_ONES
                       ).then_inc(stack0_set, 1)

            def split_parts(n, full, rest, parts, kept, chain):
                dve.wait_ge(kept, 2 * n + 2)
                dve.tensor_tensor(rest[:, :], full[:, :], parts[:, 0, :], ALU.subtract).then_inc(chain, 1)
                dve.wait_ge(chain, 3 * n + 1)
                dve.tensor_copy(parts[:, 1, :], rest[:, :]).then_inc(chain, 1)
                dve.wait_ge(chain, 3 * n + 2)
                dve.tensor_tensor(parts[:, 2, :], rest[:, :], parts[:, 1, :], ALU.subtract).then_inc(chain, 1)

            def maxima(i, ahead, t, j, tile):
                a = 16 * (G * i + ahead) + 4 * t + j
                dve.wait_ge(a_scored, a + 1)
                dve.tensor_reduce(neg_max[:, ahead % 2, NT * j + t:NT * j + t + 1], ps_a[:, tile % BANKS, :],
                                  AX.X, ALU.max, negate=True).then_inc(a_reduced, 1)

            def split_shift(i, ahead, bank):
                u = G * i + ahead
                dve.wait_ge(shift_turned, u + 1)
                if not isinstance(i, int) or u >= 1:
                    n, g = i + (ahead - 1) // G, (ahead - 1) % G
                    dve.wait_ge(shift_filled[g], 32 * n + 32)
                dve.tensor_copy(shift_parts[:, 0, :], bank[0:J * NT, 0:P]).then_inc(shift_split, 1)
                dve.wait_ge(shift_split, 2 * u + 1)
                dve.tensor_tensor(shift_parts[:, 1, :], bank[0:J * NT, 0:P], shift_parts[:, 0, :],
                                  ALU.subtract).then_inc(shift_split, 1)

            def reciprocals(n):
                dve.wait_ge(o_loaded, 32 * n + 32)
                if not isinstance(n, int) or n >= 1:
                    dve.wait_ge(recip_stored, 16 * n)
                dve.reciprocal(recips[:, :], sums[:, :]).then_inc(recip_done, 1)

            def moments(y, norm, ts, done):
                for t in ts:
                    last = dve.bn_stats(norm[0][:, t, :], y[:, t, :])
                last.then_inc(done, 1)

            def aggregate(norm, ts, aggregated):
                for t in ts:
                    last = dve.bn_aggr(norm[1][:, t, :], norm[0][:, t, :])
                last.then_inc(aggregated, 1)

            def normalize(dst, y, norm, ts, done):
                for t in ts:
                    last = dve.tensor_scalar(dst[:, t, :], y[:, t, :], norm[1][:, t, 0:1], norm[3][:, t:t + 1],
                                             ALU.subtract, ALU.mult)
                last.then_inc(done, 1)

            def residual_1(ts, bank):
                dve.tensor_tensor(y1[:, ts[0]:ts[-1] + 1, :], bank.rearrange("p (t n) -> p t n", n=P),
                                  x_biased[:, ts[0]:ts[-1] + 1, :], ALU.add).then_inc(y1_made, 1)

            def gate_product(n, c, t, bank, out):
                dve.wait_ge(tanh_done, C * n + c + 1)
                if not isinstance(n, int) or C * n + c >= 1:
                    dve.wait_ge(hidden_done, C * n + c)
                dve.scalar_tensor_tensor(out=out, in0=t, scalar=1.0, in1=bank, op0=ALU.add, op1=ALU.mult
                                         ).then_inc(gated_done, 1)

            def residual_2(n, half, bank):
                dve.wait_ge(down_made, 2 * n + half + 1)
                ts = slice(2 * half, 2 * half + 2)
                dve.tensor_tensor(y2[:, ts, :], bank[:, 2 * half * P:2 * (half + 1) * P]
                                  .rearrange("p (t n) -> p t n", t=2), x1[:, ts, :], ALU.add
                                  ).then_inc(y2_made, 1)

            def finish_rows(n):
                dve.wait_ge(rstd2_ready, n + 1)
                dve.wait_ge(result_free, 16 * n + 16)
                normalize(result, y2, norm2, range(NT), result_made)

            def gate_and_up(n, c):
                dve.wait_ge(up_made, C * n + c + 1)
                dve.wait_ge(gated_done, C * n + c + 1)
                dve.wait_ge(down_made, 2 * n)
                dve.tensor_tensor(hidden[:, c, :], gated[:, :], ps_a[:, UP_BANKS[c], :], ALU.mult).then_inc(hidden_done, 1)

            def finish_heads(g):
                dve.wait_ge(o_turned, g + 1)
                turned = ps_a[:, g % BANKS, :].rearrange("p (t j r) -> p t j r", t=NT, j=J)
                dve.reciprocal(recip_cols[:, g, :, :], turned[:, :, :, HD]).then_inc(recip_cols_made, 1)
                dve.wait_ge(recip_cols_made, g + 1)
                dve.tensor_tensor(o_rows[:, :, g * J * HD:(g + 1) * J * HD].rearrange("p t (j d) -> p t j d", j=J),
                                  turned[:, :, :, 0:HD],
                                  recip_cols[:, g, :, :].rearrange("p t (j o) -> p t j o", o=1)
                                  .to_broadcast([P, NT, J, HD]), ALU.mult).then_inc(o_rows_made, 1)

            split_parts(0, q_full, q_rest, q_parts, q_kept, q_chain)
            split_parts(0, k_full, k_rest, k_parts, k_kept, k_chain)
            dve.wait_ge(ffn_w_loaded, 48)
            for w, scale in enumerate((WEIGHT_SCALE, WEIGHT_SCALE, 0.5 * WEIGHT_SCALE)):
                dve.tensor_scalar(w_deq[:, w, :, :], w_int[:, w, :, :], scale, None, ALU.mult
                                  ).then_inc(w_scaled, 1)
            for a in range(EARLY):
                maxima(0, a // 16, a // 4 % 4, a % 4, a)
                if a == 16:
                    split_shift(0, 0, ps_b[:, 2, :])

            def batch_round(i):
                rest, post, v_ahead, proj = whole(i)
                for slot in range(G * NT):
                    g, t = slot // NT, slot % NT

                    def take(j):
                        for ahead, query, head, tile in tiles_of(i, slot, j):
                            maxima(i, ahead, query, head, tile)

                    if slot in (2, 3) and rest:
                        residual_2(i - 2, slot - 2, ps_m)
                    if slot in (4, 5) and rest:
                        if slot == 4:
                            dve.wait_ge(y2_made, 2 * (i - 1))
                        moments(y2, norm2, rows(slot - 4)[0], y2_stats)
                    if slot == 6 and post:
                        dve.wait_ge(out_made, i)
                        dve.wait_ge(x_bias_added, i)
                        residual_1(range(NT), ps_m[:, :])
                    if slot == 7 and post:
                        dve.wait_ge(y1_stats, i)
                    if slot == 8 and post:
                        dve.wait_ge(rstd1_ready, i)
                        normalize(x1, y1, norm1, range(NT), x1_made)
                    if slot == 14 and rest:
                        finish_rows(i - 2)
                    if slot == 9 and rest:
                        dve.wait_ge(y2_stats, 2 * (i - 1))
                    take(0)
                    if slot == 9 and rest:
                        aggregate(norm2, range(NT), y2_mv)
                    if slot == 7 and post:
                        aggregate(norm1, range(NT), y1_mv)
                    take(1)
                    if is_first(i) and slot in CATCH_UP_TURNS:
                        split_shift(i, CATCH_UP_TURNS.index(slot) + 1, ps_m)
                    if slot == 3 and post:
                        reciprocals(i - 1)
                    if is_last(i):
                        if slot == 9:
                            dve.wait_ge(x1T_made, LAST)
                            dve.tensor_copy(x1T[:, :], ps_m[:, :]).then_inc(x1T_kept, 1)
                        if slot in (11, 13, 15):
                            gate_and_up(LAST - 1, (11, 13, 15).index(slot))
                    gates = (10, 12, 14) if is_last(i) else (10, 13, 15)
                    if slot in gates and post:
                        gate_product(i - 1, gates.index(slot), tanh[:, :], ps_m[:, :], gated[:, :])
                    take(2)
                    if slot == 6 and post:
                        dve.wait_ge(y1_made, i)
                        moments(y1, norm1, range(NT), y1_stats)
                    turned = t == 0 and not is_first(i) and exists(i, g + 1)
                    if turned and slot == 8:
                        split_shift(i, g + 1, ps_o)
                    take(3)
                    if turned and slot != 8:
                        split_shift(i, g + 1, ps_o)
                    if is_last(i):
                        if slot == 9:
                            finish_heads(0)
                        if slot in (10, 14):
                            finish_heads((10, 14).index(slot) + 1)

            rounds(dve, batch_round)
            dve.wait_ge(down_made, 2 * (LAST - 1) + 1)
            residual_2(LAST - 1, 0, ps_m)
            finish_heads(G - 1)
            dve.wait_ge(down_made, 2 * LAST)
            residual_2(LAST - 1, 1, ps_b[:, 0, :])
            dve.wait_ge(y2_made, 2 * LAST)
            for half in range(2):
                moments(y2, norm2, rows(half)[0], y2_stats)
            dve.wait_ge(y2_stats, 2 * LAST)
            aggregate(norm2, range(NT), y2_mv)
            dve.wait_ge(x_bias_added, B)
            for half, bank in enumerate((ps_a[:, 2, :], ps_m)):
                ts, cols = rows(half)
                dve.wait_ge(out_made, LAST + half + 1)
                residual_1(ts, bank[:, cols])
                dve.wait_ge(y1_made, LAST + half + 1)
                moments(y1, norm1, ts, y1_stats)
                dve.wait_ge(y1_stats, LAST + half + 1)
                aggregate(norm1, ts, y1_mv)
            for half in range(2):
                dve.wait_ge(rstd1_ready, LAST + half + 1)
                normalize(x1, y1, norm1, rows(half)[0], x1_made)

            def gate_and_up_half(half, c):
                cols = rows(half)[1]
                n = C * (LAST + half)
                if c < C:
                    dve.wait_ge(tanh_done, n + c + 1)
                    dve.scalar_tensor_tensor(out=probs[:, 1, c, cols], in0=probs[:, 0, c, cols], scalar=1.0,
                                             in1=ps_b[:, c, cols], op0=ALU.add, op1=ALU.mult
                                             ).then_inc(gated_done, 1)
                if c > 0:
                    dve.wait_ge(up_made, n + c)
                    dve.wait_ge(gated_done, n + c)
                    dve.tensor_tensor(hidden[:, c - 1, cols], probs[:, 1, c - 1, cols], ps_a[:, c - 1, cols],
                                      ALU.mult).then_inc(hidden_done, 1)

            for half in range(2):
                for c in range(C + 1):
                    gate_and_up_half(half, c)
            dve.wait_ge(result_made, LAST)
            for half, bank in enumerate((ps_o, ps_m)):
                ts = rows(half)[0]
                residual_2(LAST, half, bank)
                dve.wait_ge(y2_made, 2 * LAST + half + 1)
                moments(y2, norm2, ts, y2_stats)
                dve.wait_ge(y2_stats, 2 * LAST + half + 1)
                aggregate(norm2, ts, y2_mv)
                if half:
                    dve.wait_ge(result_free, 16 * LAST + 16)
                    dve.wait_ge(rstd2_ready, B)
                    normalize(result, y2, norm2, rows(0)[0], result_made)
            dve.wait_ge(rstd2_ready, B + 1)
            normalize(result, y2, norm2, rows(1)[0], result_made)

        @block.gpsimd
        def _(pool):
            pool.memset(ident[:, :], 0.0).then_inc(ident_zero, 1)
            pool.wait_ge(ident_zero, 1)
            pool.affine_select(out=ident[:, :], in_=ident[:, :], compare_op=ALU.not_equal, fill=1.0, base=0,
                               pattern=[[-1, P]], channel_multiplier=1).then_inc(ident_made, 1)
            pool.memset(v_ones[:, :, :, :, :], 1.0).then_inc(const_made, 1)
            pool.memset(minus_half[:, :], -0.5).then_inc(const_made, 1)
            pool.memset(eps[:, :], EPS).then_inc(const_made, 1)
            pool.memset(one[:, :], 1.0).then_inc(const_made, 1)
            for stack, word in ((q_stack, 0.0), (k_stack, TWO_ONES)):
                pool.memset(stack[:, 1:G, :, :].rearrange("p g j s -> p (g j s)").bitcast(F32), word
                            ).then_inc(stacks_set, 1)
            pool.wait_ge(const_made, 4)
            pool.wait_ge(bias_loaded, 48)

            def split_parts(n, full, rest, parts, kept, chain):
                pool.wait_ge(kept, 2 * n + 2)
                pool.tensor_tensor(rest[:, :], full[:, :], parts[:, 0, :], ALU.subtract).then_inc(chain, 1)
                pool.wait_ge(chain, 3 * n + 1)
                pool.tensor_tensor(parts[:, 1, :], rest[:, :], one[:, :].to_broadcast([P, S]), ALU.mult
                                   ).then_inc(chain, 1)
                pool.wait_ge(chain, 3 * n + 2)
                pool.tensor_tensor(parts[:, 2, :], rest[:, :], parts[:, 1, :], ALU.subtract).then_inc(chain, 1)

            def lay_values(i, ahead):
                g = ahead % G
                cols = slice(J * HD * g, J * HD * (g + 1))
                pool.wait_ge(v_kept, i + ahead // G + 1)
                pool.tensor_tensor(v_ones[:, g, :, :, 0:HD],
                                   v_rows[:, :, cols].rearrange("p t (j d) -> p t j d", j=J),
                                   v_bias[:, cols].rearrange("p (o j d) -> p o j d", o=1, j=J)
                                   .to_broadcast([P, NT, J, HD]), ALU.add).then_inc(v_filled, 1)

            def add_out_bias(n):
                pool.wait_ge(x_reloaded, 16 * n + 16)
                if not isinstance(n, int) or n >= 1:
                    pool.wait_ge(y1_made, n)
                pool.tensor_tensor(x_biased[:, :, :], x_again[:, :, :],
                                   o_bias[:, :].rearrange("p (o n) -> p o n", o=1).to_broadcast([P, NT, P]),
                                   ALU.add).then_inc(x_bias_added, 1)

            def divide_o(n):
                pool.wait_ge(recip_loaded, 16 * n + 16)
                pool.wait_ge(o_loaded, 32 * n + 32)
                if not isinstance(n, int) or n >= 1:
                    pool.wait_ge(out_made, n)
                pool.tensor_tensor(oT_norm[:, :], oT[:, :], recip_rows[:, :], ALU.mult).then_inc(o_normed, 1)

            def inverse_deviation(n, norm, aggregated, var_ready, ready, tiles=range(NT)):
                _, mean_var, var_eps, rstd = norm
                ts = slice(tiles[0], tiles[-1] + 1)
                pool.wait_ge(aggregated, n + 1)
                pool.tensor_tensor(var_eps[:, ts], mean_var[:, ts, 1], eps[:, ts], ALU.add).then_inc(var_ready, 1)
                pool.wait_ge(var_ready, n + 1)
                pool.tensor_tensor(rstd[:, ts], var_eps[:, ts], minus_half[:, ts], ALU.pow).then_inc(ready, 1)

            def multiply_up(n, c):
                pool.wait_ge(gated_done, C * n + c + 1)
                pool.wait_ge(up_kept, C * n + c + 1)
                if c == 0 and (not isinstance(n, int) or n >= 1):
                    pool.wait_ge(down_made, 2 * n)
                pool.tensor_tensor(hidden[:, c, :], gated[:, :], up_rows[:, :], ALU.mult).then_inc(hidden_done, 1)

            for g in range(G):
                lay_values(0, g)
            for n in (1, 2):
                split_parts(n, q_full, q_rest, q_parts, q_kept, q_chain)
                split_parts(n, k_full, k_rest, k_parts, k_kept, k_chain)

            def batch_round(i):
                rest, post, v_ahead, proj = whole(i)
                for g in range(G):
                    if g == 0 and rest:
                        multiply_up(i - 2, 2)
                    if exists(i, g + 3) and not (is_first(i) and g == 0):
                        pool.wait_ge(pv_done, NT * (G * i + g))
                        lay_values(i, g + 3)
                    if g == 0 and post:
                        add_out_bias(i - 1)
                    if g == 1:
                        if post:
                            divide_o(i - 1)
                        if proj:
                            split_parts(i + 2, q_full, q_rest, q_parts, q_kept, q_chain)
                        if post:
                            inverse_deviation(i - 1, norm1, y1_mv, var1_ready, rstd1_ready)
                    if g == 2 and proj:
                        split_parts(i + 2, k_full, k_rest, k_parts, k_kept, k_chain)
                    if g == 2 and rest:
                        inverse_deviation(i - 2, norm2, y2_mv, var2_ready, rstd2_ready)
                    if is_last(i):
                        if g == 2:
                            add_out_bias(i)
                    elif g == 2 and post:
                        multiply_up(i - 1, 0)
                    elif g == 3 and post:
                        multiply_up(i - 1, 1)

            rounds(pool, batch_round)
            inverse_deviation(LAST - 1, norm2, y2_mv, var2_ready, rstd2_ready)
            for half in range(2):
                inverse_deviation(LAST + half, norm1, y1_mv, var1_ready, rstd1_ready, rows(half)[0])
            pool.wait_ge(rstd2_ready, LAST)
            pool.wait_ge(result_free, 16 * (LAST - 1) + 16)
            for t in range(NT):
                last = pool.tensor_scalar(result[:, t, :], y2[:, t, :], norm2[1][:, t, 0:1], norm2[3][:, t:t + 1],
                                          ALU.subtract, ALU.mult)
            last.then_inc(result_made, 1)
            for half in range(2):
                inverse_deviation(LAST + half, norm2, y2_mv, var2_ready, rstd2_ready, rows(half)[0])


_INS = ['L0_attn_q', 'L0_attn_in_w', 'L0_attn_qkv_bias', 'L0_attn_out_w', 'L0_attn_out_b',
        'L0_ffn_w_gate', 'L0_ffn_w_up', 'L0_ffn_w_down']


def kernel(**inputs):
    import numpy as _np
    import concourse.bacc as _bacc
    from concourse import mybir as _mybir
    from concourse.bass_utils import run_bass_kernel_spmd as _run

    nc = _bacc.Bacc("TRN2", target_bir_lowering=False, num_devices=1)
    arrays, args = {}, []
    for name in _INS:
        a = _np.ascontiguousarray(inputs[name])
        arrays[f"in_{name}_dram"] = a
        args.append(nc.dram_tensor(f"in_{name}_dram", a.shape, _mybir.dt.from_np(a.dtype), kind="ExternalInput").ap())
    shape = inputs['L0_attn_q'].shape
    out = nc.dram_tensor("out_0_dram", shape, _mybir.dt.from_np(_np.dtype('float32')), kind="ExternalOutput").ap()
    transformer_layer(nc, *args, out)
    r = _run(nc, [arrays], core_ids=[0])
    return r.results[0]["out_0_dram"]
```
